# Optimizing a Trainium2 kernel written in Bass

```python
import numpy as np
import jax
import jax.numpy as jnp

def _softmax(x, axis=-1):
    return jax.nn.softmax(x, axis=axis)

def _gelu(x):
    return jax.nn.gelu(x, approximate=True)

def _silu(x):
    return jax.nn.silu(x)

def _sigmoid(x):
    return jax.nn.sigmoid(x)

def _layernorm(x, axis=-1, eps=1e-05):
    m = jnp.mean(x, axis=axis, keepdims=True)
    v = jnp.var(x, axis=axis, keepdims=True)
    return (x - m) / jnp.sqrt(v + eps)

def _scatter_add(tgt, idx, src, axis=0):
    return tgt.at[idx].add(src)

def _segment_sum(src, seg, n):
    return jax.ops.segment_sum(src, seg, n)
kernel_name = 'mk_conv_seq_d1_conv_nchw256_r2_0d813c'

def setup_inputs(seed: int=0):
    np.random.seed(seed)
    _w = jnp.asarray

    def _rec_inputs():
        import jax
        import jax.numpy as jnp
        _gk = jax.random.key(seed)
        x = 7.22e-05 + 1 * jax.random.normal(jax.random.fold_in(_gk, 1), (8, 128, 32, 32), jnp.float32)
        return x
    x = _rec_inputs()

    def _L0_conv_setup():
        import jax, jax.numpy as jnp
        import numpy as np
        B, C, H, W = (8, 128, 32, 32)
        GROUPS = 32
        EPS = 1e-05

        def group_norm(x, w, b):
            Bn, Cn, Hn, Wn = x.shape
            xg = x.reshape(Bn, GROUPS, Cn // GROUPS, Hn, Wn)
            mu = jnp.mean(xg, axis=(2, 3, 4), keepdims=True)
            var = jnp.var(xg, axis=(2, 3, 4), keepdims=True)
            xn = (xg - mu) * jax.lax.rsqrt(var + EPS)
            xn = xn.reshape(Bn, Cn, Hn, Wn)
            return xn * w[None, :, None, None] + b[None, :, None, None]
        key = jax.random.key(seed)
        ks = jax.random.split(key, 6)
        s = 1.0 / np.sqrt(C)
        return {'x': jax.random.normal(ks[0], (B, C, H, W), dtype=jnp.float32), 'gn_w': jnp.ones((C,), jnp.float32), 'gn_b': jnp.zeros((C,), jnp.float32), 'wq': jax.random.normal(ks[1], (C, C), jnp.float32) * s, 'bq': jnp.zeros((C,), jnp.float32), 'wk': jax.random.normal(ks[2], (C, C), jnp.float32) * s, 'bk': jnp.zeros((C,), jnp.float32), 'wv': jax.random.normal(ks[3], (C, C), jnp.float32) * s, 'bv': jnp.zeros((C,), jnp.float32), 'wo': jax.random.normal(ks[4], (C, C), jnp.float32) * s, 'bo': jnp.zeros((C,), jnp.float32)}
    _L0_conv_all = _L0_conv_setup()
    _L0_conv_in = {k: v for k, v in _L0_conv_all.items() if k in ('gn_w', 'gn_b', 'wq', 'bq', 'wk', 'bk', 'wv', 'bv', 'wo', 'bo')}
    del _L0_conv_all
    return {'x': x, 'L0_conv_gn_w': _L0_conv_in['gn_w'], 'L0_conv_gn_b': _L0_conv_in['gn_b'], 'L0_conv_wq': _L0_conv_in['wq'], 'L0_conv_bq': _L0_conv_in['bq'], 'L0_conv_wk': _L0_conv_in['wk'], 'L0_conv_bk': _L0_conv_in['bk'], 'L0_conv_wv': _L0_conv_in['wv'], 'L0_conv_bv': _L0_conv_in['bv'], 'L0_conv_wo': _L0_conv_in['wo'], 'L0_conv_bo': _L0_conv_in['bo']}

def reference(x, L0_conv_gn_w, L0_conv_gn_b, L0_conv_wq, L0_conv_bq, L0_conv_wk, L0_conv_bk, L0_conv_wv, L0_conv_bv, L0_conv_wo, L0_conv_bo):
    import jax
    import jax.numpy as jnp

    def _L0_conv_ref(x, gn_w, gn_b, wq, bq, wk, bk, wv, bv, wo, bo):
        import jax, jax.numpy as jnp
        import numpy as np
        B, C, H, W = (8, 128, 32, 32)
        GROUPS = 32
        EPS = 1e-05

        def group_norm(x, w, b):
            Bn, Cn, Hn, Wn = x.shape
            xg = x.reshape(Bn, GROUPS, Cn // GROUPS, Hn, Wn)
            mu = jnp.mean(xg, axis=(2, 3, 4), keepdims=True)
            var = jnp.var(xg, axis=(2, 3, 4), keepdims=True)
            xn = (xg - mu) * jax.lax.rsqrt(var + EPS)
            xn = xn.reshape(Bn, Cn, Hn, Wn)
            return xn * w[None, :, None, None] + b[None, :, None, None]
        Bn, Cn, Hn, Wn = x.shape
        h = group_norm(x, gn_w, gn_b)
        hf = h.reshape(Bn, Cn, Hn * Wn)
        q = jnp.einsum('bcn,oc->bno', hf, wq) + bq
        k = jnp.einsum('bcn,oc->bon', hf, wk) + bk[None, :, None]
        v = jnp.einsum('bcn,oc->bno', hf, wv) + bv
        alpha = jnp.einsum('bnc,bcm->bnm', q, k) / jnp.sqrt(jnp.float32(Cn))
        alpha = jax.nn.softmax(alpha, axis=-1)
        out = jnp.einsum('bnm,bmc->bnc', alpha, v)
        out = jnp.einsum('bnc,oc->bon', out, wo) + bo[None, :, None]
        return out.reshape(Bn, Cn, Hn, Wn) + x

    def _gn(v, G=32, eps=1e-05):
        B_, C_, H_, W_ = v.shape
        g = v.reshape(B_, G, C_ // G, H_, W_)
        m = jnp.mean(g, axis=(2, 3, 4), keepdims=True)
        s = jnp.var(g, axis=(2, 3, 4), keepdims=True)
        return ((g - m) / jnp.sqrt(s + eps)).reshape(v.shape)

    def _ln_c(v, eps=1e-06):
        m = jnp.mean(v, axis=1, keepdims=True)
        s = jnp.var(v, axis=1, keepdims=True)
        return (v - m) / jnp.sqrt(s + eps)

    def _ln_t(v, eps=1e-05):
        m = jnp.mean(v, axis=-1, keepdims=True)
        s = jnp.var(v, axis=-1, keepdims=True)
        return (v - m) / jnp.sqrt(s + eps)

    def _to_tokens(v):
        B_, C_, H_, W_ = v.shape
        return v.reshape(B_, C_, H_ * W_).transpose(0, 2, 1)

    def _from_tokens(t, like):
        B_, C_, H_, W_ = like.shape
        return t.transpose(0, 2, 1).reshape(B_, C_, H_, W_)
    x = _L0_conv_ref(x, L0_conv_gn_w, L0_conv_gn_b, L0_conv_wq, L0_conv_bq, L0_conv_wk, L0_conv_bk, L0_conv_wv, L0_conv_bv, L0_conv_wo, L0_conv_bo)
    return x

_drawn_inputs = setup_inputs


def setup_inputs(seed=0):
    import zlib

    import numpy as np

    out = dict(_drawn_inputs(seed))
    spreads = {'L0_conv_gn_w': (1.0, 0.2),
     'L0_conv_gn_b': (0.0, 0.1),
     'L0_conv_bq': (0.0, 0.8),
     'L0_conv_bk': (0.0, 0.8),
     'L0_conv_bv': (0.0, 0.1),
     'L0_conv_bo': (0.0, 0.1)}
    factors = {}
    for name, (base, spread) in spreads.items():
        noise = np.random.default_rng([zlib.crc32(name.encode()), seed]).standard_normal(out[name].shape)
        drawn = base * np.exp(spread * noise) if base else spread * noise
        out[name] = jnp.asarray(drawn.astype(out[name].dtype))
    for name, factor in factors.items():
        out[name] = (out[name] * factor).astype(out[name].dtype)
    return out
```

```python
import concourse.bass as bass
from concourse import mybir
from contextlib import ExitStack


def groupnorm_attention_kernel(
    nc: bass.Bass,
    x: bass.AP,
    gn_w: bass.AP,
    gn_b: bass.AP,
    wq: bass.AP,
    bq: bass.AP,
    wk: bass.AP,
    bk: bass.AP,
    wv: bass.AP,
    bv: bass.AP,
    wo: bass.AP,
    bo: bass.AP,
    out: bass.AP,
):
    fp32, fp16 = mybir.dt.float32, mybir.dt.float16
    ALU = mybir.AluOpType
    ACT = mybir.ActivationFunctionType
    AX = mybir.AxisListType

    B, C, HH, WW = x.shape
    N = HH * WW
    GROUPS = 32
    GC = C // GROUPS
    EPS = 1e-5
    SCALE = float(C) ** -0.5
    TILES = N // 128
    GT = 4
    GN = GT * 128
    HALF = 512
    P_SCALE = 4096.0
    VW = C + 1
    V_PARTS = [(0, 3), (3, 3), (6, 2)]
    NV = len(V_PARTS)

    x_d = x.rearrange("b c h w -> b c (h w)")
    out_d = out.rearrange("b c h w -> b c (h w)")

    ctx = ExitStack()
    with ctx:
        def sb(name, shape, dt):
            return ctx.enter_context(nc.sbuf_tensor(name, shape, dt))

        def pb(name, shape, dt):
            return ctx.enter_context(nc.psum_tensor(name, shape, dt))

        def sem(name):
            return ctx.enter_context(nc.semaphore(name))

        wq_sb, wk_sb, wv_sb, wo_sb = (sb(n, [C, C], fp32) for n in ("wq_sb", "wk_sb", "wv_sb", "wo_sb"))
        gw, gb, bq_sb, bk_sb, bv_sb, bo_sb = (
            sb(n, [C, 1], fp32) for n in ("gw", "gb", "bq_sb", "bk_sb", "bv_sb", "bo_sb"))
        ident = sb("ident", [128, 128], fp32)
        neg_mean_mat = sb("neg_mean_mat", [C, C], fp32)
        mean_mat = sb("mean_mat", [C, C], fp32)
        woT = sb("woT", [C, C], fp32)
        wu = sb("wu", [C, C], fp32)
        wu_hi, wu_lo = sb("wu_hi", [C, C], fp16), sb("wu_lo", [C, C], fp16)
        wvc = sb("wvc", [C, VW], fp32)
        wvc_hi, wvc_lo = sb("wvc_hi", [C, VW], fp16), sb("wvc_lo", [C, VW], fp16)
        ub = sb("ub", [C, 1], fp32)
        cb = sb("cb", [128, 1], fp32)
        obias = sb("obias", [C, 1], fp32)

        x_sb = sb("x_sb", [C, 2, N], fp32)
        xres = sb("xres", [C, 2, N], fp32)
        bn6 = sb("bn6", [C, 2, 2, 6], fp32)
        mv = sb("mv", [C, 2, 2], fp32)
        neg_mean = sb("neg_mean", [C, 2], fp32)
        dmean = sb("dmean", [C, 2], fp32)
        spread = sb("spread", [C, 2], fp32)
        var_eps = sb("var_eps", [C, 2], fp32)
        ln_var = sb("ln_var", [C, 2], fp32)
        rstd0 = sb("rstd0", [C, 2], fp32)
        newton = sb("newton", [C, 2, 2], fp32)
        ga, gc = sb("ga", [C, 2], fp32), sb("gc", [C, 2], fp32)
        hx, h = sb("hx", [C, N], fp32), sb("h", [C, N], fp32)
        zero = sb("zero", [C, 1], fp32)
        h_hi, h_lo = sb("h_hi", [C, 2, N], fp16), sb("h_lo", [C, 2, N], fp16)
        u_hi, u_lo = sb("u_hi", [C, 2, N], fp16), sb("u_lo", [C, 2, N], fp16)
        v_hi, v_lo = sb("v_hi", [128, 2, TILES, VW], fp16), sb("v_lo", [128, 2, TILES, VW], fp16)
        c_tok = sb("c_tok", [128, 2, TILES], fp32)

        neg_max = sb("neg_max", [128, 2, TILES], fp32)
        exp_bias = sb("exp_bias", [128, 2, TILES], fp32)
        row_sum = sb("row_sum", [128, 2, TILES], fp32)
        scaled_sum = sb("scaled_sum", [128, 2, GT], fp32)
        row_inv = sb("row_inv", [128, 2, GT], fp32)
        probs = sb("probs", [128, 2, N], fp32)
        pT_hi = sb("pT_hi", [128, 2, TILES, GT, 128], fp16)
        pT_lo = sb("pT_lo", [128, 2, TILES, GT, 128], fp16)
        inv_rows = sb("inv_rows", [128, GN], fp32)
        attn = sb("attn", [C, 2, GN], fp32)
        y = sb("y", [C, 2, GN], fp32)

        S = [pb(f"S{i}", [128, N], fp32) for i in range(2)]
        pT = [pb(f"pT{i}", [128, GT, 128], fp32) for i in range(2)]
        O = pb("O", [C, GN], fp32)
        misc = pb("misc", [128, HALF], fp32)

        wqk_in, wvo_in, vec_in = sem("wqk_in"), sem("wvo_in"), sem("vec_in")
        x_in = [sem(f"x_in{p}") for p in range(2)]
        y_out = [sem(f"y_out{q}") for q in range(2)]
        pool_step = sem("pool_step")
        consts = sem("consts")
        wprod = sem("wprod")
        wcopy = sem("wcopy")
        wstep = sem("wstep")
        stats = sem("stats")
        mean_mm, var_mm = sem("mean_mm"), sem("var_mm")
        mean_out = sem("mean_out")
        var_out = sem("var_out")
        ln_step = sem("ln_step")
        rstd_ready = sem("rstd_ready")
        affine = sem("affine")
        h_step = sem("h_step")
        h_ready = sem("h_ready")
        xres_done = sem("xres_done")
        u_mm, v_mm = sem("u_mm"), sem("v_mm")
        u_hi_done, v_hi_done = sem("u_hi_done"), sem("v_hi_done")
        u_done, v_done = sem("u_done"), sem("v_done")
        c_done = sem("c_done")
        qk_done = sem("qk_done")
        max_step = sem("max_step")
        bias_done = sem("bias_done")
        exp_done = sem("exp_done")
        tr_done = sem("tr_done")
        hi_done = sem("hi_done")
        lo_done = sem("lo_done")
        av_done = sem("av_done")
        inv_step = sem("inv_step")
        inv_done = sem("inv_done")
        inv_mm = sem("inv_mm")
        inv_out = sem("inv_out")
        attn_done = sem("attn_done")
        y_done = sem("y_done")

        block = ctx.enter_context(nc.Block())

        def turn(r, p, d):
            return r + (p + d) // 2

        def group_of(b, j):
            past = j - 5
            d = -1 if past < 0 else 0
            q = (past // GT) % 2
            return q, d, 2 * (b + d) + q, past % GT

        @block.sync
        def _(eng):
            def load_x(b, p):
                eng.dma_start(x_sb[:, p, :], x_d[b, :, :]).then_inc(x_in[p], 16)

            def store(b, q):
                eng.wait_ge(y_done, 2 * b + q + 1)
                eng.dma_start(out_d[b, :, q * GN:(q + 1) * GN], y[:, q, :]).then_inc(y_out[q], 16)

            def batch(b, p, load):
                if not (isinstance(b, int) and b == 0):
                    store(b - 1, 0)
                    store(b - 1, 1)
                if load:
                    eng.wait_ge(xres_done, b + 2)
                    load_x(b + 3, 1 - p)

            load_x(0, 0)
            load_x(1, 1)
            eng.wait_ge(xres_done, 1)
            load_x(2, 0)
            batch(0, 0, True)
            with eng.Fori(0, (B - 4) // 2) as i:
                batch(2 * i + 1, 1, True)
                batch(2 * i + 2, 0, True)
            for b in range(B - 3, B):
                batch(b, b % 2, False)
            store(B - 1, 0)
            store(B - 1, 1)
            for q in range(2):
                eng.wait_ge(y_out[q], 16 * B)

        @block.gpsimd
        def _(eng):
            nc.gpsimd.memset(ident[:, :], 0.0).then_inc(pool_step, 1)
            nc.gpsimd.memset(neg_mean_mat[:, :], -1.0 / GC).then_inc(pool_step, 1)
            nc.gpsimd.memset(mean_mat[:, :], 1.0 / GC).then_inc(pool_step, 1)
            nc.gpsimd.memset(zero[:, :], 0.0).then_inc(pool_step, 1)
            eng.wait_ge(pool_step, 4)
            nc.gpsimd.affine_select(out=ident[:, :], in_=ident[:, :], compare_op=ALU.not_equal, fill=1.0,
                                    base=0, pattern=[[-1, 128]], channel_multiplier=1).then_inc(consts, 1)
            for m in (neg_mean_mat, mean_mat):
                nc.gpsimd.affine_select(out=m[:, :], in_=m[:, :], compare_op=ALU.is_ge, fill=0.0,
                                        base=0, pattern=[[-GC, GROUPS], [0, GC]],
                                        channel_multiplier=1).then_inc(pool_step, 1)
            eng.wait_ge(pool_step, 6)
            for m in (neg_mean_mat, mean_mat):
                nc.gpsimd.affine_select(out=m[:, :], in_=m[:, :], compare_op=ALU.is_ge, fill=0.0,
                                        base=GC - 1, pattern=[[GC, GROUPS], [0, GC]],
                                        channel_multiplier=-1).then_inc(consts, 1)

            def normalise(b, p, r, first):
                eng.wait_ge(affine, b + 1)
                if not first:
                    eng.wait_ge(qk_done, (b - 1) * TILES)
                nc.gpsimd.tensor_tensor(hx[:, :], x_sb[:, p, :], ga[:, p:p + 1].to_broadcast([C, N]),
                                        ALU.mult).then_inc(h_step, 1)
                eng.wait_ge(h_step, 3 * b + 1)
                nc.gpsimd.tensor_tensor(h[:, :], hx[:, :], gc[:, p:p + 1].to_broadcast([C, N]),
                                        ALU.add).then_inc(h_step, 1)
                eng.wait_ge(h_step, 3 * b + 2)
                nc.gpsimd.tensor_tensor(h_hi[:, p, :], h[:, :], zero[:, :].to_broadcast([C, N]),
                                        ALU.add).then_inc(h_step, 1)
                eng.wait_ge(h_step, 3 * b + 3)
                nc.gpsimd.tensor_tensor(h_lo[:, p, :], h[:, :], h_hi[:, p, :], ALU.subtract).then_inc(h_ready, 1)

            def residual(b, p):
                nc.gpsimd.tensor_tensor(xres[:, p, :], x_sb[:, p, :], obias[:, :].to_broadcast([C, N]),
                                        ALU.add).then_inc(xres_done, 1)

            def result(b, p, q, first):
                eng.wait_ge(attn_done, 2 * b + q + 1)
                eng.wait_ge(xres_done, b + 1)
                if not first:
                    eng.wait_ge(y_out[q], 16 * b)
                nc.gpsimd.tensor_tensor(y[:, q, :], attn[:, q, :], xres[:, p, q * GN:(q + 1) * GN],
                                        ALU.add).then_inc(y_done, 1)

            def batch(b, p, r, after_first, after_second, last):
                if after_first:
                    result(b - 1, 1 - p, 0, not after_second)
                if not last:
                    normalise(b + 1, 1 - p, turn(r, p, 1), not after_first)
                if after_first:
                    result(b - 1, 1 - p, 1, not after_second)
                if not last:
                    if after_first:
                        eng.wait_ge(y_done, 2 * b)
                    residual(b + 1, 1 - p)

            normalise(0, 0, 0, True)
            eng.wait_ge(wcopy, 7)
            residual(0, 0)
            batch(0, 0, 0, False, False, False)
            batch(1, 1, 0, True, False, False)
            batch(2, 0, 1, True, True, False)
            with eng.Fori(1, (B - 2) // 2) as i:
                batch(2 * i + 1, 1, i, True, True, False)
                batch(2 * i + 2, 0, i + 1, True, True, False)
            batch(B - 1, 1, B // 2 - 1, True, True, True)
            result(B - 1, 1, 0, False)
            result(B - 1, 1, 1, False)

        @block.tensor
        def _(pe):
            def product(i, outs):
                if i:
                    pe.wait_ge(wcopy, i)
                for o, l, r in outs:
                    last = nc.tensor.matmul(o, l, r, start=True, stop=True)
                last.then_inc(wprod, 1)

            pe.wait_ge(wqk_in, 32)
            product(0, [(misc[:, 0:C], wq_sb[:, :], wk_sb[:, :])])
            pe.wait_ge(vec_in, 96)
            product(1, [(misc[:, 0:1], wk_sb[:, :], bq_sb[:, :])])
            product(2, [(misc[:, 0:1], wq_sb[:, :], bk_sb[:, :])])
            product(3, [(misc[:, 0:1], bq_sb[:, 0:1].to_broadcast([C, 128]), bk_sb[:, :])])
            pe.wait_ge(wvo_in, 32)
            pe.wait_ge(consts, 3)
            pe.wait_ge(wcopy, 4)
            nc.tensor.transpose(misc[:, 0:C], wo_sb[:, :], ident[:, :]).then_inc(wprod, 1)
            product(5, [(misc[:, 0:C], wv_sb[:, :], woT[:, :])])
            product(6, [(misc[:, 0:1], woT[:, :], bv_sb[:, :])])

            def split_product(o, l_hi, l_lo, r_hi, r_lo):
                nc.tensor.matmul(o, l_hi, r_hi, start=True, stop=False)
                nc.tensor.matmul(o, l_hi, r_lo, start=False, stop=False)
                return nc.tensor.matmul(o, l_lo, r_hi, start=False, stop=True)

            def group_mean(b, p):
                pe.wait_ge(stats, b + 1)
                nc.tensor.matmul(misc[:, 0:1], neg_mean_mat[:, :], mv[:, p, 0:1],
                                 start=True, stop=True).then_inc(mean_mm, 1)

            def group_var(b, p):
                pe.wait_ge(mean_out, b + 1)
                nc.tensor.matmul(misc[:, 0:1], mean_mat[:, :], spread[:, p:p + 1],
                                 start=True, stop=True).then_inc(var_mm, 1)

            def project_u(b, p, half):
                pe.wait_ge(h_ready, b + 1)
                if half:
                    pe.wait_ge(u_done, 2 * b + 1)
                cols = slice(half * HALF, (half + 1) * HALF)
                split_product(misc[:, :], wu_hi[:, :], wu_lo[:, :], h_hi[:, p, cols],
                              h_lo[:, p, cols]).then_inc(u_mm, 1)

            def project_v(b, p, part):
                if part:
                    pe.wait_ge(c_done, NV * b + part)
                else:
                    pe.wait_ge(u_done, 2 * b + 2)
                t0, n = V_PARTS[part]
                for k in range(n):
                    tok = slice((t0 + k) * 128, (t0 + k + 1) * 128)
                    last = split_product(misc[:, k * VW:(k + 1) * VW], h_hi[:, p, tok], h_lo[:, p, tok],
                                         wvc_hi[:, :], wvc_lo[:, :])
                last.then_inc(v_mm, 1)

            def inverse_rows(b, q):
                pe.wait_ge(inv_done, 2 * b + q + 1)
                for t in range(GT):
                    last = nc.tensor.transpose(misc[:, t * 128:(t + 1) * 128],
                                               row_inv[:, q, t:t + 1].to_broadcast([128, 128]), ident[:, :])
                last.then_inc(inv_mm, 1)

            def logits(b, p, n, first):
                T = TILES * b + n
                if n == 0:
                    pe.wait_ge(u_done, 2 * b + 1)
                if n == GT:
                    pe.wait_ge(u_done, 2 * b + 2)
                if not first:
                    pe.wait_ge(exp_done, T - 1)
                s, q_hi, q_lo = S[n % 2], u_hi[:, p, n * 128:(n + 1) * 128], u_lo[:, p, n * 128:(n + 1) * 128]
                halves = [slice(c * HALF, (c + 1) * HALF) for c in range(N // HALF)]
                for c in halves:
                    nc.tensor.matmul(s[:, c], q_hi, h_hi[:, p, c], start=True, stop=False)
                for c in halves:
                    nc.tensor.matmul(s[:, c], q_hi, h_lo[:, p, c], start=False, stop=False)
                for c in halves:
                    last = nc.tensor.matmul(s[:, c], q_lo, h_hi[:, p, c], start=False, stop=True)
                last.then_inc(qk_done, 1)

            def values(b, j, p, first_group):
                q, d, g, k = group_of(b, j)
                pv = (p + d) % 2
                if k == 0:
                    pe.wait_ge(lo_done, 2 * GT * (g + 1))
                    if q == 0:
                        pe.wait_ge(v_done, NV * (b + d + 1))
                    if not first_group:
                        pe.wait_ge(attn_done, g)
                for m in (2 * k, 2 * k + 1):
                    vh, vl = v_hi[:, pv, m, 0:C], v_lo[:, pv, m, 0:C]
                    ph = pT_hi[:, q, m, :, :].rearrange("p t n -> p (t n)")
                    pl = pT_lo[:, q, m, :, :].rearrange("p t n -> p (t n)")
                    nc.tensor.matmul(O[:, :], vh, ph, start=(m == 0), stop=False)
                    nc.tensor.matmul(O[:, :], vh, pl, start=False, stop=False)
                    last = nc.tensor.matmul(O[:, :], vl, ph, start=False, stop=(m == TILES - 1))
                last.then_inc(av_done, 1)

            def transposes(b, n, first):
                T = TILES * b + n
                pe.wait_ge(exp_done, T + 1)
                for half in range(2):
                    if not first:
                        pe.wait_ge(lo_done, 2 * T - 1 + half)
                    for t in range(GT):
                        m = half * GT + t
                        last = nc.tensor.transpose(pT[half][:, t, :], probs[:, n % 2, m * 128:(m + 1) * 128],
                                                   ident[:, :])
                    last.then_inc(tr_done, 1)

            def batch(b, p, first, last):
                for j in range(TILES):
                    if j < TILES - 1:
                        logits(b, p, j + 1, first and j == 0)
                    elif not last:
                        logits(b + 1, 1 - p, 0, False)
                    if j == 7 and not last:
                        project_v(b + 1, 1 - p, 2)
                    if not first or j >= 5:
                        values(b, j, p, first and j == 5)
                    if not last:
                        if j == 0:
                            if not first:
                                pe.wait_ge(inv_out, 2 * b - 1)
                            group_mean(b + 1, 1 - p)
                        if j == 1:
                            group_var(b + 1, 1 - p)
                    if j == 2 and not first:
                        if not last:
                            pe.wait_ge(var_out, b + 2)
                        else:
                            pe.wait_ge(inv_out, 2 * b - 1)
                        inverse_rows(b - 1, 1)
                    if not last:
                        if j == 3:
                            if not first:
                                pe.wait_ge(inv_out, 2 * b)
                            project_u(b + 1, 1 - p, 0)
                        if j == 4:
                            project_u(b + 1, 1 - p, 1)
                        if j == 5:
                            project_v(b + 1, 1 - p, 0)
                        if j == 6:
                            project_v(b + 1, 1 - p, 1)
                    if j == 7:
                        if not last:
                            pe.wait_ge(c_done, NV * (b + 2))
                        else:
                            pe.wait_ge(inv_out, 2 * b)
                        inverse_rows(b, 0)
                    transposes(b, j, first and j == 0)

            pe.wait_ge(wcopy, 7)
            group_mean(0, 0)
            group_var(0, 0)
            pe.wait_ge(wcopy, 8)
            project_u(0, 0, 0)
            project_u(0, 0, 1)
            for part in range(NV):
                project_v(0, 0, part)
            logits(0, 0, 0, True)
            pe.wait_ge(c_done, NV)
            batch(0, 0, True, False)
            with pe.Fori(0, (B - 2) // 2) as i:
                batch(2 * i + 1, 1, False, False)
                batch(2 * i + 2, 0, False, False)
            batch(B - 1, 1, False, True)
            values(B, 0, 0, False)
            for j in range(1, 5):
                values(B, j, 0, False)
                if j == 1:
                    pe.wait_ge(inv_out, 2 * B - 1)
                    inverse_rows(B - 1, 1)

        @block.scalar
        def _(act):
            for dst, src in ((wq_sb, wq), (wk_sb, wk)):
                act.dma_start(dst[:, :], src).then_inc(wqk_in, 16)
            for dst, src in ((bq_sb, bq), (bk_sb, bk), (bv_sb, bv), (bo_sb, bo), (gw, gn_w), (gb, gn_b)):
                act.dma_start(dst[:, :], src.rearrange("(c one) -> c one", one=1)).then_inc(vec_in, 16)
            for dst, src in ((wv_sb, wv), (wo_sb, wo)):
                act.dma_start(dst[:, :], src).then_inc(wvo_in, 16)

            def u_high(b, p, half):
                act.wait_ge(u_mm, 2 * b + half + 1)
                nc.scalar.activation(u_hi[:, p, half * HALF:(half + 1) * HALF], misc[:, :], ACT.Identity,
                                     bias=ub[:, :]).then_inc(u_hi_done, 1)

            def v_high(b, p, part):
                t0, n = V_PARTS[part]
                act.wait_ge(v_mm, NV * b + part + 1)
                nc.scalar.copy(v_hi[:, p, t0:t0 + n, :].rearrange("p t c -> p (t c)"),
                               misc[:, 0:n * VW]).then_inc(v_hi_done, 1)

            def inverse_copy(b, q, first):
                act.wait_ge(inv_mm, 2 * b + q + 1)
                if not first:
                    act.wait_ge(attn_done, 2 * b + q)
                nc.scalar.copy(inv_rows[:, :], misc[:, :]).then_inc(inv_out, 1)

            def inverse_deviation(b, p):
                act.wait_ge(var_out, b + 1)
                nc.scalar.activation(ln_var[:, p:p + 1], var_eps[:, p:p + 1], ACT.Ln).then_inc(ln_step, 1)
                act.wait_ge(ln_step, b + 1)
                nc.scalar.activation(rstd0[:, p:p + 1], ln_var[:, p:p + 1], ACT.Exp,
                                     scale=-0.5).then_inc(rstd_ready, 1)

            def exponentials(b, p, n, first):
                T = TILES * b + n
                act.wait_ge(bias_done, T + 1)
                if not first:
                    act.wait_ge(tr_done, 2 * T - 2)
                nc.scalar.activation(probs[:, n % 2, :], S[n % 2][:, :], ACT.Exp, bias=exp_bias[:, p, n:n + 1],
                                     accum_out=row_sum[:, p, n:n + 1]).then_inc(exp_done, 1)

            def high_parts(b, p, n, free):
                T = TILES * b + n
                g = n // GT
                for half in range(2):
                    act.wait_ge(tr_done, 2 * T + half + 1)
                    if n % GT == 0 and half == 0 and free:
                        act.wait_ge(av_done, GT * (2 * b + g - 1))
                    nc.scalar.activation(pT_hi[:, g, half * GT:(half + 1) * GT, n % GT, :], pT[half][:, :, :],
                                         ACT.Copy, scale=P_SCALE).then_inc(hi_done, 1)

            def batch(b, p, first, last):
                for j in range(TILES):
                    high_parts(b, p, j, not first)
                    if j < TILES - 1:
                        exponentials(b, p, j + 1, first and j == 0)
                    elif not last:
                        exponentials(b + 1, 1 - p, 0, False)
                    if j == 2 and not first:
                        inverse_copy(b - 1, 1, False)
                    if not last:
                        if j == 1:
                            inverse_deviation(b + 1, 1 - p)
                        if j == 3:
                            u_high(b + 1, 1 - p, 0)
                        if j == 4:
                            u_high(b + 1, 1 - p, 1)
                        if j == 5:
                            v_high(b + 1, 1 - p, 0)
                        if j == 6:
                            v_high(b + 1, 1 - p, 1)
                            v_high(b + 1, 1 - p, 2)
                    if j == 7:
                        inverse_copy(b, 0, first)

            inverse_deviation(0, 0)
            u_high(0, 0, 0)
            u_high(0, 0, 1)
            for part in range(NV):
                v_high(0, 0, part)
            exponentials(0, 0, 0, True)
            batch(0, 0, True, False)
            with act.Fori(0, (B - 2) // 2) as i:
                batch(2 * i + 1, 1, False, False)
                batch(2 * i + 2, 0, False, False)
            batch(B - 1, 1, False, True)
            inverse_copy(B - 1, 1, False)

        @block.vector
        def _(dve):
            wsteps = [0]

            def linked(ins):
                wsteps[0] += 1
                ins.then_inc(wstep, 1)
                dve.wait_ge(wstep, wsteps[0])

            dve.wait_ge(wprod, 1)
            nc.vector.tensor_scalar(wu[:, :], misc[:, 0:C], SCALE, None, ALU.mult).then_inc(wcopy, 1)
            dve.wait_ge(wprod, 2)
            nc.vector.tensor_scalar(ub[:, :], misc[:, 0:1], SCALE, None, ALU.mult).then_inc(wcopy, 1)
            dve.wait_ge(wprod, 3)
            nc.vector.tensor_scalar(wvc[:, C:C + 1], misc[:, 0:1], SCALE, None, ALU.mult).then_inc(wcopy, 1)
            dve.wait_ge(wprod, 4)
            nc.vector.tensor_scalar(cb[:, :], misc[:, 0:1], SCALE, None, ALU.mult).then_inc(wcopy, 1)
            dve.wait_ge(wprod, 5)
            nc.vector.tensor_copy(woT[:, :], misc[:, 0:C]).then_inc(wcopy, 1)
            dve.wait_ge(wprod, 6)
            nc.vector.tensor_copy(wvc[:, 0:C], misc[:, 0:C]).then_inc(wcopy, 1)
            dve.wait_ge(wprod, 7)
            nc.vector.tensor_scalar(obias[:, :], misc[:, 0:1], bo_sb[:, :], None, ALU.add).then_inc(wcopy, 1)
            dve.wait_ge(wcopy, 7)
            nc.vector.tensor_copy(wu_hi[:, :], wu[:, :])
            linked(nc.vector.tensor_copy(wvc_hi[:, :], wvc[:, :]))
            nc.vector.tensor_tensor(wu_lo[:, :], wu[:, :], wu_hi[:, :], ALU.subtract)
            linked(nc.vector.tensor_tensor(wvc_lo[:, :], wvc[:, :], wvc_hi[:, :], ALU.subtract))
            WEIGHT_STEPS = wsteps[0]

            STAT_STEPS, MEAN_STEPS, VAR_STEPS = 2, 2, 3

            def at(b, k):
                return (STAT_STEPS + MEAN_STEPS + VAR_STEPS) * b + (WEIGHT_STEPS + k)

            def channel_stats(b, p, r):
                dve.wait_ge(x_in[p], 16 * r + 16)
                for c in range(2):
                    last = nc.vector.bn_stats(bn6[:, p, c, :], x_sb[:, p, c * HALF:(c + 1) * HALF])
                    last.then_inc(wstep, 1)

            def aggregate(b, p):
                nc.vector.bn_aggr(mv[:, p, :], bn6[:, p, :, :].rearrange("p c s -> p (c s)")).then_inc(stats, 1)

            def group_spread(b, p):
                dve.wait_ge(mean_mm, b + 1)
                nc.vector.tensor_copy(neg_mean[:, p:p + 1], misc[:, 0:1]).then_inc(wstep, 1)
                nc.vector.tensor_tensor(dmean[:, p:p + 1], misc[:, 0:1], mv[:, p, 0:1], ALU.add).then_inc(wstep, 1)
                dve.wait_ge(wstep, at(b, 4))
                nc.vector.scalar_tensor_tensor(out=spread[:, p:p + 1], in0=dmean[:, p:p + 1],
                                               scalar=dmean[:, p:p + 1], in1=mv[:, p, 1:2],
                                               op0=ALU.mult, op1=ALU.add).then_inc(mean_out, 1)

            def variance_out(b, p):
                dve.wait_ge(var_mm, b + 1)
                nc.vector.tensor_scalar(var_eps[:, p:p + 1], misc[:, 0:1], EPS, None, ALU.add).then_inc(var_out, 1)

            def group_affine(b, p):
                dve.wait_ge(rstd_ready, b + 1)
                r0 = rstd0[:, p:p + 1]
                nc.vector.scalar_tensor_tensor(out=newton[:, p, 0:1], in0=r0, scalar=r0, in1=var_eps[:, p:p + 1],
                                               op0=ALU.mult, op1=ALU.mult).then_inc(wstep, 1)
                dve.wait_ge(wstep, at(b, 5))
                nc.vector.tensor_scalar(newton[:, p, 1:2], newton[:, p, 0:1], -0.5, 1.5,
                                        ALU.mult, ALU.add).then_inc(wstep, 1)
                dve.wait_ge(wstep, at(b, 6))
                nc.vector.scalar_tensor_tensor(out=ga[:, p:p + 1], in0=r0, scalar=newton[:, p, 1:2], in1=gw[:, :],
                                               op0=ALU.mult, op1=ALU.mult).then_inc(wstep, 1)
                dve.wait_ge(wstep, at(b, 7))
                nc.vector.scalar_tensor_tensor(out=gc[:, p:p + 1], in0=neg_mean[:, p:p + 1],
                                               scalar=ga[:, p:p + 1], in1=gb[:, :],
                                               op0=ALU.mult, op1=ALU.add).then_inc(affine, 1)

            def u_low(b, p, half):
                cols = slice(half * HALF, (half + 1) * HALF)
                dve.wait_ge(u_hi_done, 2 * b + half + 1)
                nc.vector.scalar_tensor_tensor(out=u_lo[:, p, cols], in0=misc[:, :], scalar=ub[:, :],
                                               in1=u_hi[:, p, cols], op0=ALU.add,
                                               op1=ALU.subtract).then_inc(u_done, 1)

            def v_low(b, p, part):
                t0, n = V_PARTS[part]
                dve.wait_ge(v_hi_done, NV * b + part + 1)
                nc.vector.tensor_tensor(v_lo[:, p, t0:t0 + n, :].rearrange("p t c -> p (t c)"), misc[:, 0:n * VW],
                                        v_hi[:, p, t0:t0 + n, :].rearrange("p t c -> p (t c)"),
                                        ALU.subtract).then_inc(v_done, 1)
                nc.vector.tensor_scalar(c_tok[:, p, t0:t0 + n],
                                        misc[:, 0:n * VW].rearrange("p (t c) -> p t c", c=VW)[:, :, C],
                                        cb[:, :], None, ALU.add).then_inc(c_done, 1)

            def tile_max(b, p, n):
                T = TILES * b + n
                dve.wait_ge(qk_done, T + 1)
                nc.vector.tensor_reduce(out=neg_max[:, p, n:n + 1], in_=S[n % 2][:, :], axis=AX.X, op=ALU.max,
                                        negate=True).then_inc(max_step, 1)
                dve.wait_ge(max_step, T + 1)
                if n in (0, 3, 6):
                    dve.wait_ge(c_done, NV * b + n // 3 + 1)
                nc.vector.tensor_scalar(exp_bias[:, p, n:n + 1], neg_max[:, p, n:n + 1], c_tok[:, p, n:n + 1],
                                        c_tok[:, p, n:n + 1], ALU.subtract, ALU.add).then_inc(bias_done, 1)

            def low_parts(b, n):
                T = TILES * b + n
                g = n // GT
                for half in range(2):
                    dve.wait_ge(hi_done, 2 * T + half + 1)
                    ms = slice(half * GT, (half + 1) * GT)
                    nc.vector.scalar_tensor_tensor(out=pT_lo[:, g, ms, n % GT, :], in0=pT[half][:, :, :],
                                                   scalar=P_SCALE, in1=pT_hi[:, g, ms, n % GT, :],
                                                   op0=ALU.mult, op1=ALU.subtract).then_inc(lo_done, 1)

            def reciprocals(b, p, q):
                dve.wait_ge(exp_done, TILES * b + GT * (q + 1))
                nc.vector.tensor_scalar(scaled_sum[:, q, :], row_sum[:, p, q * GT:(q + 1) * GT], P_SCALE, None,
                                        ALU.mult).then_inc(inv_step, 1)
                dve.wait_ge(inv_step, 2 * b + q + 1)
                nc.vector.reciprocal(row_inv[:, q, :], scaled_sum[:, q, :]).then_inc(inv_done, 1)

            def normalised(b, q, first):
                dve.wait_ge(av_done, GT * (2 * b + q + 1))
                dve.wait_ge(inv_out, 2 * b + q + 1)
                if not first:
                    dve.wait_ge(y_done, 2 * b + q - 1)
                nc.vector.tensor_tensor(attn[:, q, :], O[:, :], inv_rows[:, :], ALU.mult).then_inc(attn_done, 1)

            def batch(b, p, r, first, second, last):
                for j in range(TILES):
                    if j == 0 and not last:
                        channel_stats(b + 1, 1 - p, turn(r, p, 1))
                        dve.wait_ge(wstep, at(b + 1, 2))
                    if j < TILES - 1:
                        tile_max(b, p, j + 1)
                    elif not last:
                        tile_max(b + 1, 1 - p, 0)
                    if j == 0 and not last:
                        aggregate(b + 1, 1 - p)
                    if j == 0 and not first:
                        normalised(b - 1, 0, second)
                        reciprocals(b - 1, 1 - p, 1)
                    if j == 1 and not last:
                        group_spread(b + 1, 1 - p)
                    if j == 4 and not first:
                        normalised(b - 1, 1, second)
                    low_parts(b, j)
                    if not last:
                        if j == 1:
                            variance_out(b + 1, 1 - p)
                        if j == 2:
                            group_affine(b + 1, 1 - p)
                        if j == 3:
                            u_low(b + 1, 1 - p, 0)
                        if j == 4:
                            u_low(b + 1, 1 - p, 1)
                        if j == 5:
                            v_low(b + 1, 1 - p, 0)
                        if j == 6:
                            v_low(b + 1, 1 - p, 1)
                            v_low(b + 1, 1 - p, 2)
                    if j == 5:
                        reciprocals(b, p, 0)

            channel_stats(0, 0, 0)
            dve.wait_ge(wstep, at(0, 2))
            aggregate(0, 0)
            group_spread(0, 0)
            variance_out(0, 0)
            group_affine(0, 0)
            nc.vector.drain().then_inc(wcopy, 1)
            u_low(0, 0, 0)
            u_low(0, 0, 1)
            for part in range(NV):
                v_low(0, 0, part)
            tile_max(0, 0, 0)
            batch(0, 0, 0, True, False, False)
            batch(1, 1, 0, False, True, False)
            batch(2, 0, 1, False, False, False)
            with dve.Fori(1, (B - 2) // 2) as i:
                batch(2 * i + 1, 1, i, False, False, False)
                batch(2 * i + 2, 0, i + 1, False, False, False)
            batch(B - 1, 1, B // 2 - 1, False, False, True)
            reciprocals(B - 1, 1, 1)
            normalised(B - 1, 0, False)
            normalised(B - 1, 1, False)


_INS = ['x', 'L0_conv_gn_w', 'L0_conv_gn_b', 'L0_conv_wq', 'L0_conv_bq', 'L0_conv_wk', 'L0_conv_bk',
        'L0_conv_wv', 'L0_conv_bv', 'L0_conv_wo', 'L0_conv_bo']
_OUTS = [((8, 128, 32, 32), 'float32')]


def kernel(**inputs):
    import numpy as _np
    import concourse.bacc as _bacc
    from concourse import mybir as _mybir
    from concourse.bass_utils import run_bass_kernel_spmd as _run

    nc = _bacc.Bacc("TRN2", target_bir_lowering=False, num_devices=1)
    arrays, args = {}, []
    for name in _INS:
        a = _np.ascontiguousarray(inputs[name])
        arrays[f"in_{name}_dram"] = a
        args.append(nc.dram_tensor(f"in_{name}_dram", a.shape, _mybir.dt.from_np(a.dtype), kind="ExternalInput").ap())
    for i, (shape, dtype) in enumerate(_OUTS):
        dt = _mybir.dt.from_np(_np.dtype(dtype))
        args.append(nc.dram_tensor(f"out_{i}_dram", shape, dt, kind="ExternalOutput").ap())
    groupnorm_attention_kernel(nc, *args)
    r = _run(nc, [arrays], core_ids=[0])
    return r.results[0]["out_0_dram"]
```

```python
import concourse.bass as bass
from concourse import mybir
from contextlib import ExitStack


def groupnorm_attention_kernel(
    nc: bass.Bass,
    x: bass.AP,
    gn_w: bass.AP,
    gn_b: bass.AP,
    wq: bass.AP,
    bq: bass.AP,
    wk: bass.AP,
    bk: bass.AP,
    wv: bass.AP,
    bv: bass.AP,
    wo: bass.AP,
    bo: bass.AP,
    out: bass.AP,
):
    fp32, fp16 = mybir.dt.float32, mybir.dt.float16
    ALU = mybir.AluOpType
    ACT = mybir.ActivationFunctionType
    AX = mybir.AxisListType

    B, C, HH, WW = x.shape
    N = HH * WW
    GROUPS = 32
    GC = C // GROUPS
    EPS = 1e-5
    SCALE = float(C) ** -0.5
    TILES = N // 128
    GT = 4
    GN = GT * 128
    HALF = 512
    P_SCALE = 4096.0
    VW = C + 1
    V_PARTS = [(0, 3), (3, 3), (6, 2)]
    NV = len(V_PARTS)

    x_d = x.rearrange("b c h w -> b c (h w)")
    out_d = out.rearrange("b c h w -> b c (h w)")

    ctx = ExitStack()
    with ctx:
        def sb(name, shape, dt):
            return ctx.enter_context(nc.sbuf_tensor(name, shape, dt))

        def pb(name, shape, dt):
            return ctx.enter_context(nc.psum_tensor(name, shape, dt))

        def sem(name):
            return ctx.enter_context(nc.semaphore(name))

        wq_sb, wk_sb, wv_sb, wo_sb = (sb(n, [C, C], fp32) for n in ("wq_sb", "wk_sb", "wv_sb", "wo_sb"))
        gw, gb, bq_sb, bk_sb, bv_sb, bo_sb = (
            sb(n, [C, 1], fp32) for n in ("gw", "gb", "bq_sb", "bk_sb", "bv_sb", "bo_sb"))
        ident = sb("ident", [128, 128], fp32)
        neg_mean_mat = sb("neg_mean_mat", [C, C], fp32)
        mean_mat = sb("mean_mat", [C, C], fp32)
        woT = sb("woT", [C, C], fp32)
        wu = sb("wu", [C, C], fp32)
        wu_hi, wu_lo = sb("wu_hi", [C, C], fp16), sb("wu_lo", [C, C], fp16)
        wvc = sb("wvc", [C, VW], fp32)
        wvc_hi, wvc_lo = sb("wvc_hi", [C, VW], fp16), sb("wvc_lo", [C, VW], fp16)
        ub = sb("ub", [C, 1], fp32)
        cb = sb("cb", [128, 1], fp32)
        obias = sb("obias", [C, 1], fp32)

        x_sb = sb("x_sb", [C, 2, N], fp32)
        xres = sb("xres", [C, 2, N], fp32)
        bn6 = sb("bn6", [C, 2, 2, 6], fp32)
        mv = sb("mv", [C, 2, 2], fp32)
        neg_mean = sb("neg_mean", [C, 2], fp32)
        dmean = sb("dmean", [C, 2], fp32)
        spread = sb("spread", [C, 2], fp32)
        var_eps = sb("var_eps", [C, 2], fp32)
        ln_var = sb("ln_var", [C, 2], fp32)
        rstd0 = sb("rstd0", [C, 2], fp32)
        newton = sb("newton", [C, 2, 2], fp32)
        ga, gc = sb("ga", [C, 2], fp32), sb("gc", [C, 2], fp32)
        h = sb("h", [C, N], fp32)
        zero = sb("zero", [128, 1], fp32)
        zeros = sb("zeros", [128, 3, C], fp32)
        h_hi, h_lo = sb("h_hi", [C, 2, N], fp16), sb("h_lo", [C, 2, N], fp16)
        u = sb("u", [C, N], fp32)
        v = sb("v", [128, TILES, VW], fp32)
        u_hi, u_lo = sb("u_hi", [C, 2, N], fp16), sb("u_lo", [C, 2, N], fp16)
        v_hi, v_lo = sb("v_hi", [128, 2, TILES, C], fp16), sb("v_lo", [128, 2, TILES, C], fp16)
        c_tok = sb("c_tok", [128, 2, TILES], fp32)

        neg_max = sb("neg_max", [128, 2, TILES], fp32)
        exp_bias = sb("exp_bias", [128, 2, TILES], fp32)
        row_sum = sb("row_sum", [128, 2, TILES], fp32)
        scaled_sum = sb("scaled_sum", [128, 2, GT], fp32)
        row_inv = sb("row_inv", [128, 2, GT], fp32)
        probs = sb("probs", [128, 2, N], fp32)
        pT_hi = sb("pT_hi", [128, 2, TILES, GT, 128], fp16)
        pT_lo = sb("pT_lo", [128, 2, TILES, GT, 128], fp16)
        inv_rows = sb("inv_rows", [C, 2, GN], fp32)
        av = sb("av", [C, 2, GN], fp32)
        attn = sb("attn", [C, 2, GN], fp32)
        y = sb("y", [C, 2, GN], fp32)

        S = [pb(f"S{i}", [128, N], fp32) for i in range(2)]
        pT = [pb(f"pT{i}", [128, GT, 128], fp32) for i in range(2)]
        O = pb("O", [C, GN], fp32)
        misc = pb("misc", [128, HALF], fp32)

        wqk_in, wvo_in, vec_in = sem("wqk_in"), sem("wvo_in"), sem("vec_in")
        x_in = [sem(f"x_in{p}") for p in range(2)]
        y_out = [sem(f"y_out{q}") for q in range(2)]
        pool_step = sem("pool_step")
        consts = sem("consts")
        wprod = sem("wprod")
        wcopy = sem("wcopy")
        wstep = sem("wstep")
        stats = sem("stats")
        mean_mm, var_mm = sem("mean_mm"), sem("var_mm")
        mean_out = sem("mean_out")
        var_out = sem("var_out")
        ln_step = sem("ln_step")
        rstd_ready = sem("rstd_ready")
        affine = sem("affine")
        h_done = sem("h_done")
        h_step = sem("h_step")
        h_ready = sem("h_ready")
        xres_done = sem("xres_done")
        u_mm, v_mm = sem("u_mm"), sem("v_mm")
        u_out, v_out = sem("u_out"), sem("v_out")
        u_step, v_step = sem("u_step"), sem("v_step")
        u_done, v_done = sem("u_done"), sem("v_done")
        c_done = sem("c_done")
        qk_done = sem("qk_done")
        max_step = sem("max_step")
        bias_done = sem("bias_done")
        exp_done = sem("exp_done")
        tr_done = sem("tr_done")
        hi_done = sem("hi_done")
        lo_done = sem("lo_done")
        av_done = sem("av_done")
        inv_step = sem("inv_step")
        inv_done = sem("inv_done")
        inv_mm = sem("inv_mm")
        inv_out = sem("inv_out")
        av_out = sem("av_out")
        attn_done = sem("attn_done")
        y_done = sem("y_done")

        block = ctx.enter_context(nc.Block())

        def turn(r, p, d):
            return r + (p + d) // 2

        def group_of(b, j):
            past = j - 5
            d = -1 if past < 0 else 0
            q = (past // GT) % 2
            return q, d, 2 * (b + d) + q, past % GT

        @block.sync
        def _(eng):
            def load_x(b, p):
                eng.dma_start(x_sb[:, p, :], x_d[b, :, :]).then_inc(x_in[p], 16)

            def store(b, q):
                eng.wait_ge(y_done, 2 * b + q + 1)
                eng.dma_start(out_d[b, :, q * GN:(q + 1) * GN], y[:, q, :]).then_inc(y_out[q], 16)

            def batch(b, p, load):
                if not (isinstance(b, int) and b == 0):
                    store(b - 1, 0)
                    store(b - 1, 1)
                if load:
                    eng.wait_ge(xres_done, b + 2)
                    load_x(b + 3, 1 - p)

            load_x(0, 0)
            load_x(1, 1)
            eng.wait_ge(xres_done, 1)
            load_x(2, 0)
            batch(0, 0, True)
            with eng.Fori(0, (B - 4) // 2) as i:
                batch(2 * i + 1, 1, True)
                batch(2 * i + 2, 0, True)
            for b in range(B - 3, B):
                batch(b, b % 2, False)
            store(B - 1, 0)
            store(B - 1, 1)
            for q in range(2):
                eng.wait_ge(y_out[q], 16 * B)

        @block.gpsimd
        def _(eng):
            nc.gpsimd.memset(ident[:, :], 0.0).then_inc(pool_step, 1)
            nc.gpsimd.memset(neg_mean_mat[:, :], -1.0 / GC).then_inc(pool_step, 1)
            nc.gpsimd.memset(mean_mat[:, :], 1.0 / GC).then_inc(pool_step, 1)
            nc.gpsimd.memset(zero[:, :], 0.0).then_inc(pool_step, 1)
            nc.gpsimd.memset(zeros[:, :, :], 0.0).then_inc(pool_step, 1)
            eng.wait_ge(pool_step, 5)
            nc.gpsimd.affine_select(out=ident[:, :], in_=ident[:, :], compare_op=ALU.not_equal, fill=1.0,
                                    base=0, pattern=[[-1, 128]], channel_multiplier=1).then_inc(consts, 1)
            for m in (neg_mean_mat, mean_mat):
                nc.gpsimd.affine_select(out=m[:, :], in_=m[:, :], compare_op=ALU.is_ge, fill=0.0,
                                        base=0, pattern=[[-GC, GROUPS], [0, GC]],
                                        channel_multiplier=1).then_inc(pool_step, 1)
            eng.wait_ge(pool_step, 7)
            for m in (neg_mean_mat, mean_mat):
                nc.gpsimd.affine_select(out=m[:, :], in_=m[:, :], compare_op=ALU.is_ge, fill=0.0,
                                        base=GC - 1, pattern=[[GC, GROUPS], [0, GC]],
                                        channel_multiplier=-1).then_inc(consts, 1)

            def h_parts(b, p, first):
                eng.wait_ge(h_done, b + 1)
                if not first:
                    eng.wait_ge(qk_done, (b - 1) * TILES)
                nc.gpsimd.tensor_tensor(h_hi[:, p, :], h[:, :], zero[:, :].to_broadcast([C, N]),
                                        ALU.add).then_inc(h_step, 1)
                eng.wait_ge(h_step, b + 1)
                nc.gpsimd.tensor_tensor(h_lo[:, p, :], h[:, :], h_hi[:, p, :], ALU.subtract).then_inc(h_ready, 1)

            def u_parts(b, p, half):
                cols = slice(half * HALF, (half + 1) * HALF)
                eng.wait_ge(u_out, 2 * b + half + 1)
                nc.gpsimd.tensor_tensor(u_hi[:, p, cols], u[:, cols], zero[:, :].to_broadcast([C, HALF]),
                                        ALU.add).then_inc(u_step, 1)
                eng.wait_ge(u_step, 2 * b + half + 1)
                nc.gpsimd.tensor_tensor(u_lo[:, p, cols], u[:, cols], u_hi[:, p, cols],
                                        ALU.subtract).then_inc(u_done, 1)

            def v_parts(b, p, part, first):
                t0, n = V_PARTS[part]
                eng.wait_ge(v_out, NV * b + part + 1)
                nc.gpsimd.tensor_tensor(c_tok[:, p, t0:t0 + n], v[:, t0:t0 + n, C],
                                        cb[:, :].to_broadcast([128, n]), ALU.add).then_inc(c_done, 1)
                if part == 0 and not first:
                    eng.wait_ge(av_done, TILES * (b - 1))
                nc.gpsimd.tensor_tensor(v_hi[:, p, t0:t0 + n, :], v[:, t0:t0 + n, 0:C],
                                        zeros[:, 0:n, :], ALU.add).then_inc(v_step, 1)
                eng.wait_ge(v_step, NV * b + part + 1)
                nc.gpsimd.tensor_tensor(v_lo[:, p, t0:t0 + n, :], v[:, t0:t0 + n, 0:C],
                                        v_hi[:, p, t0:t0 + n, :], ALU.subtract).then_inc(v_done, 1)

            def residual(b, p):
                nc.gpsimd.tensor_tensor(xres[:, p, :], x_sb[:, p, :], obias[:, :].to_broadcast([C, N]),
                                        ALU.add).then_inc(xres_done, 1)

            def result(b, p, q, first):
                g = 2 * b + q
                eng.wait_ge(inv_out, g + 1)
                eng.wait_ge(av_out, g + 1)
                nc.gpsimd.tensor_tensor(attn[:, q, :], av[:, q, :], inv_rows[:, q, :], ALU.mult).then_inc(attn_done, 1)
                eng.wait_ge(xres_done, b + 1)
                eng.wait_ge(attn_done, g + 1)
                if not first:
                    eng.wait_ge(y_out[q], 16 * b)
                nc.gpsimd.tensor_tensor(y[:, q, :], attn[:, q, :], xres[:, p, q * GN:(q + 1) * GN],
                                        ALU.add).then_inc(y_done, 1)

            def batch(b, p, after_first, after_second, last):
                u_parts(b, p, 1)
                v_parts(b, p, 1, False)
                if after_first:
                    result(b - 1, 1 - p, 0, not after_second)
                if not last:
                    h_parts(b + 1, 1 - p, not after_first)
                v_parts(b, p, 2, False)
                if not last:
                    u_parts(b + 1, 1 - p, 0)
                    v_parts(b + 1, 1 - p, 0, not after_first)
                if after_first:
                    result(b - 1, 1 - p, 1, not after_second)
                if not last:
                    if after_first:
                        eng.wait_ge(y_done, 2 * b)
                    residual(b + 1, 1 - p)

            h_parts(0, 0, True)
            u_parts(0, 0, 0)
            v_parts(0, 0, 0, True)
            eng.wait_ge(wcopy, 7)
            residual(0, 0)
            batch(0, 0, False, False, False)
            batch(1, 1, True, False, False)
            batch(2, 0, True, True, False)
            with eng.Fori(1, (B - 2) // 2) as i:
                batch(2 * i + 1, 1, True, True, False)
                batch(2 * i + 2, 0, True, True, False)
            batch(B - 1, 1, True, True, True)
            result(B - 1, 1, 0, False)
            result(B - 1, 1, 1, False)

        @block.tensor
        def _(pe):
            def product(i, outs):
                if i:
                    pe.wait_ge(wcopy, i)
                for o, l, r in outs:
                    last = nc.tensor.matmul(o, l, r, start=True, stop=True)
                last.then_inc(wprod, 1)

            pe.wait_ge(wqk_in, 32)
            product(0, [(misc[:, 0:C], wq_sb[:, :], wk_sb[:, :])])
            pe.wait_ge(vec_in, 96)
            product(1, [(misc[:, 0:1], wk_sb[:, :], bq_sb[:, :])])
            product(2, [(misc[:, 0:1], wq_sb[:, :], bk_sb[:, :])])
            product(3, [(misc[:, 0:1], bq_sb[:, 0:1].to_broadcast([C, 128]), bk_sb[:, :])])
            pe.wait_ge(wvo_in, 32)
            pe.wait_ge(consts, 3)
            pe.wait_ge(wcopy, 4)
            nc.tensor.transpose(misc[:, 0:C], wo_sb[:, :], ident[:, :]).then_inc(wprod, 1)
            product(5, [(misc[:, 0:C], wv_sb[:, :], woT[:, :])])
            product(6, [(misc[:, 0:1], woT[:, :], bv_sb[:, :])])

            def split_product(o, l_hi, l_lo, r_hi, r_lo):
                nc.tensor.matmul(o, l_hi, r_hi, start=True, stop=False)
                nc.tensor.matmul(o, l_hi, r_lo, start=False, stop=False)
                return nc.tensor.matmul(o, l_lo, r_hi, start=False, stop=True)

            def group_mean(b, p):
                pe.wait_ge(stats, b + 1)
                nc.tensor.matmul(misc[:, 0:1], neg_mean_mat[:, :], mv[:, p, 0:1],
                                 start=True, stop=True).then_inc(mean_mm, 1)

            def group_var(b, p):
                pe.wait_ge(mean_out, b + 1)
                nc.tensor.matmul(misc[:, 0:1], mean_mat[:, :], spread[:, p:p + 1],
                                 start=True, stop=True).then_inc(var_mm, 1)

            def project_u(b, p, half):
                pe.wait_ge(h_ready, b + 1)
                cols = slice(half * HALF, (half + 1) * HALF)
                split_product(misc[:, :], wu_hi[:, :], wu_lo[:, :], h_hi[:, p, cols],
                              h_lo[:, p, cols]).then_inc(u_mm, 1)

            def project_v(b, p, part):
                t0, n = V_PARTS[part]
                for k in range(n):
                    tok = slice((t0 + k) * 128, (t0 + k + 1) * 128)
                    last = split_product(misc[:, k * VW:(k + 1) * VW], h_hi[:, p, tok], h_lo[:, p, tok],
                                         wvc_hi[:, :], wvc_lo[:, :])
                last.then_inc(v_mm, 1)

            def inverse_rows(b, q):
                pe.wait_ge(inv_done, 2 * b + q + 1)
                for t in range(GT):
                    last = nc.tensor.transpose(misc[:, t * 128:(t + 1) * 128],
                                               row_inv[:, q, t:t + 1].to_broadcast([128, 128]), ident[:, :])
                last.then_inc(inv_mm, 1)

            def logits(b, p, n, first):
                T = TILES * b + n
                if n == 0:
                    pe.wait_ge(u_done, 2 * b + 1)
                if n == GT:
                    pe.wait_ge(u_done, 2 * b + 2)
                if not first:
                    pe.wait_ge(exp_done, T - 1)
                s, q_hi, q_lo = S[n % 2], u_hi[:, p, n * 128:(n + 1) * 128], u_lo[:, p, n * 128:(n + 1) * 128]
                halves = [slice(c * HALF, (c + 1) * HALF) for c in range(N // HALF)]
                for c in halves:
                    nc.tensor.matmul(s[:, c], q_hi, h_hi[:, p, c], start=True, stop=False)
                for c in halves:
                    nc.tensor.matmul(s[:, c], q_hi, h_lo[:, p, c], start=False, stop=False)
                for c in halves:
                    last = nc.tensor.matmul(s[:, c], q_lo, h_hi[:, p, c], start=False, stop=True)
                last.then_inc(qk_done, 1)

            def values(b, j, p, first_group):
                q, d, g, k = group_of(b, j)
                pv = (p + d) % 2
                if k == 0:
                    pe.wait_ge(lo_done, 2 * GT * (g + 1))
                    if q == 0:
                        pe.wait_ge(v_done, NV * (b + d + 1))
                    if not first_group:
                        pe.wait_ge(av_out, g)
                for m in (2 * k, 2 * k + 1):
                    vh, vl = v_hi[:, pv, m, 0:C], v_lo[:, pv, m, 0:C]
                    ph = pT_hi[:, q, m, :, :].rearrange("p t n -> p (t n)")
                    pl = pT_lo[:, q, m, :, :].rearrange("p t n -> p (t n)")
                    nc.tensor.matmul(O[:, :], vh, ph, start=(m == 0), stop=False)
                    nc.tensor.matmul(O[:, :], vh, pl, start=False, stop=False)
                    last = nc.tensor.matmul(O[:, :], vl, ph, start=False, stop=(m == TILES - 1))
                last.then_inc(av_done, 1)

            def transposes(b, n, first):
                T = TILES * b + n
                pe.wait_ge(exp_done, T + 1)
                for half in range(2):
                    if not first:
                        pe.wait_ge(lo_done, 2 * T - 1 + half)
                    for t in range(GT):
                        m = half * GT + t
                        last = nc.tensor.transpose(pT[half][:, t, :], probs[:, n % 2, m * 128:(m + 1) * 128],
                                                   ident[:, :])
                    last.then_inc(tr_done, 1)

            def batch(b, p, first, last):
                np = 1 - p
                for j in range(TILES):
                    if j < TILES - 1:
                        logits(b, p, j + 1, first and j == 0)
                    elif not last:
                        logits(b + 1, np, 0, False)
                    if j == 1:
                        pe.wait_ge(u_out, 2 * b + 2)
                        project_v(b, p, 1)
                    if j == 5 and not last:
                        pe.wait_ge(v_out, NV * b + 3)
                        project_u(b + 1, np, 0)
                    if j == 6 and not last:
                        pe.wait_ge(u_out, 2 * b + 3)
                        project_v(b + 1, np, 0)
                    if not first or j >= 5:
                        values(b, j, p, first and j == 5)
                    if j == 0:
                        if first:
                            pe.wait_ge(v_out, 1)
                        else:
                            pe.wait_ge(inv_out, 2 * b - 1)
                        project_u(b, p, 1)
                    if j == 1 and not last:
                        pe.wait_ge(v_out, NV * b + 2)
                        group_mean(b + 1, np)
                    if j == 2 and not last:
                        group_var(b + 1, np)
                    if j == 3 and not first:
                        if last:
                            pe.wait_ge(v_out, NV * b + 2)
                        else:
                            pe.wait_ge(var_out, b + 2)
                        inverse_rows(b - 1, 1)
                    if j == 4:
                        if first:
                            pe.wait_ge(var_out, b + 2)
                        else:
                            pe.wait_ge(inv_out, 2 * b)
                        project_v(b, p, 2)
                    if j == 7:
                        pe.wait_ge(v_out, NV * b + (3 if last else 4))
                        inverse_rows(b, 0)
                    transposes(b, j, first and j == 0)

            pe.wait_ge(wcopy, 7)
            group_mean(0, 0)
            group_var(0, 0)
            pe.wait_ge(wcopy, 8)
            project_u(0, 0, 0)
            pe.wait_ge(u_out, 1)
            project_v(0, 0, 0)
            logits(0, 0, 0, True)
            batch(0, 0, True, False)
            with pe.Fori(0, (B - 2) // 2) as i:
                batch(2 * i + 1, 1, False, False)
                batch(2 * i + 2, 0, False, False)
            batch(B - 1, 1, False, True)
            values(B, 0, 0, False)
            for j in range(1, 5):
                values(B, j, 0, False)
                if j == 1:
                    pe.wait_ge(inv_out, 2 * B - 1)
                    inverse_rows(B - 1, 1)

        @block.scalar
        def _(act):
            for dst, src in ((wq_sb, wq), (wk_sb, wk)):
                act.dma_start(dst[:, :], src).then_inc(wqk_in, 16)
            for dst, src in ((bq_sb, bq), (bk_sb, bk), (bv_sb, bv), (bo_sb, bo), (gw, gn_w), (gb, gn_b)):
                act.dma_start(dst[:, :], src.rearrange("(c one) -> c one", one=1)).then_inc(vec_in, 16)
            for dst, src in ((wv_sb, wv), (wo_sb, wo)):
                act.dma_start(dst[:, :], src).then_inc(wvo_in, 16)

            def copy_u(b, half, first):
                act.wait_ge(u_mm, 2 * b + half + 1)
                if not first:
                    act.wait_ge(u_done, 2 * b + half - 1)
                nc.scalar.activation(u[:, half * HALF:(half + 1) * HALF], misc[:, :], ACT.Identity,
                                     bias=ub[:, :]).then_inc(u_out, 1)

            def copy_v(b, part, first):
                t0, n = V_PARTS[part]
                act.wait_ge(v_mm, NV * b + part + 1)
                if not first:
                    act.wait_ge(v_done, NV * (b - 1) + part + 1)
                nc.scalar.copy(v[:, t0:t0 + n, :].rearrange("p t c -> p (t c)"),
                               misc[:, 0:n * VW]).then_inc(v_out, 1)

            def copy_inverse(b, q, first):
                act.wait_ge(inv_mm, 2 * b + q + 1)
                if not first:
                    act.wait_ge(attn_done, 2 * b + q - 1)
                nc.scalar.copy(inv_rows[:, q, :], misc[:, :]).then_inc(inv_out, 1)

            def copy_values(b, q, first):
                act.wait_ge(av_done, GT * (2 * b + q + 1))
                if not first:
                    act.wait_ge(attn_done, 2 * b + q - 1)
                nc.scalar.copy(av[:, q, :], O[:, :]).then_inc(av_out, 1)

            def inverse_deviation(b, p):
                act.wait_ge(var_out, b + 1)
                nc.scalar.activation(ln_var[:, p:p + 1], var_eps[:, p:p + 1], ACT.Ln).then_inc(ln_step, 1)
                act.wait_ge(ln_step, b + 1)
                nc.scalar.activation(rstd0[:, p:p + 1], ln_var[:, p:p + 1], ACT.Exp,
                                     scale=-0.5).then_inc(rstd_ready, 1)

            def exponentials(b, p, n, first):
                T = TILES * b + n
                act.wait_ge(bias_done, T + 1)
                if not first:
                    act.wait_ge(tr_done, 2 * T - 2)
                nc.scalar.activation(probs[:, n % 2, :], S[n % 2][:, :], ACT.Exp, bias=exp_bias[:, p, n:n + 1],
                                     accum_out=row_sum[:, p, n:n + 1]).then_inc(exp_done, 1)

            def high_parts(b, p, n, free):
                T = TILES * b + n
                g = n // GT
                for half in range(2):
                    act.wait_ge(tr_done, 2 * T + half + 1)
                    if n % GT == 0 and half == 0 and free:
                        act.wait_ge(av_done, GT * (2 * b + g - 1))
                    nc.scalar.activation(pT_hi[:, g, half * GT:(half + 1) * GT, n % GT, :], pT[half][:, :, :],
                                         ACT.Copy, scale=P_SCALE).then_inc(hi_done, 1)

            def batch(b, p, first, second, last):
                for j in range(TILES):
                    if j == 0:
                        if not first:
                            copy_values(b - 1, 0, second)
                        copy_u(b, 1, first)
                    if j == 1:
                        copy_v(b, 1, first)
                    if j == 2 and not last:
                        inverse_deviation(b + 1, 1 - p)
                    if j == 3 and not first:
                        copy_inverse(b - 1, 1, second)
                    if j == 4:
                        if not first:
                            copy_values(b - 1, 1, second)
                        copy_v(b, 2, first)
                    if j == 5 and not last:
                        copy_u(b + 1, 0, False)
                    if j == 6 and not last:
                        copy_v(b + 1, 0, False)
                    if j == 7:
                        copy_inverse(b, 0, first)
                    high_parts(b, p, j, not first)
                    if j < TILES - 1:
                        exponentials(b, p, j + 1, first and j == 0)
                    elif not last:
                        exponentials(b + 1, 1 - p, 0, False)

            nc.scalar.preload_act_table_set("natural_log_exp_and_others")
            inverse_deviation(0, 0)
            copy_u(0, 0, True)
            copy_v(0, 0, True)
            exponentials(0, 0, 0, True)
            batch(0, 0, True, False, False)
            batch(1, 1, False, True, False)
            batch(2, 0, False, False, False)
            with act.Fori(1, (B - 2) // 2) as i:
                batch(2 * i + 1, 1, False, False, False)
                batch(2 * i + 2, 0, False, False, False)
            batch(B - 1, 1, False, False, True)
            copy_values(B - 1, 0, False)
            copy_inverse(B - 1, 1, False)
            copy_values(B - 1, 1, False)

        @block.vector
        def _(dve):
            wsteps = [0]

            def linked(ins):
                wsteps[0] += 1
                ins.then_inc(wstep, 1)
                dve.wait_ge(wstep, wsteps[0])

            dve.wait_ge(wprod, 1)
            nc.vector.tensor_scalar(wu[:, :], misc[:, 0:C], SCALE, None, ALU.mult).then_inc(wcopy, 1)
            dve.wait_ge(wprod, 2)
            nc.vector.tensor_scalar(ub[:, :], misc[:, 0:1], SCALE, None, ALU.mult).then_inc(wcopy, 1)
            dve.wait_ge(wprod, 3)
            nc.vector.tensor_scalar(wvc[:, C:C + 1], misc[:, 0:1], SCALE, None, ALU.mult).then_inc(wcopy, 1)
            dve.wait_ge(wprod, 4)
            nc.vector.tensor_scalar(cb[:, :], misc[:, 0:1], SCALE, None, ALU.mult).then_inc(wcopy, 1)
            dve.wait_ge(wprod, 5)
            nc.vector.tensor_copy(woT[:, :], misc[:, 0:C]).then_inc(wcopy, 1)
            dve.wait_ge(wprod, 6)
            nc.vector.tensor_copy(wvc[:, 0:C], misc[:, 0:C]).then_inc(wcopy, 1)
            dve.wait_ge(wprod, 7)
            nc.vector.tensor_scalar(obias[:, :], misc[:, 0:1], bo_sb[:, :], None, ALU.add).then_inc(wcopy, 1)
            dve.wait_ge(wcopy, 7)
            nc.vector.tensor_copy(wu_hi[:, :], wu[:, :])
            linked(nc.vector.tensor_copy(wvc_hi[:, :], wvc[:, :]))
            nc.vector.tensor_tensor(wu_lo[:, :], wu[:, :], wu_hi[:, :], ALU.subtract)
            nc.vector.tensor_tensor(wvc_lo[:, :], wvc[:, :], wvc_hi[:, :], ALU.subtract).then_inc(wcopy, 1)
            WEIGHT_STEPS = wsteps[0]

            STAT_STEPS, MEAN_STEPS, VAR_STEPS = 2, 2, 3

            def at(b, k):
                return (STAT_STEPS + MEAN_STEPS + VAR_STEPS) * b + (WEIGHT_STEPS + k)

            def channel_stats(b, p, r):
                dve.wait_ge(x_in[p], 16 * r + 16)
                for c in range(2):
                    last = nc.vector.bn_stats(bn6[:, p, c, :], x_sb[:, p, c * HALF:(c + 1) * HALF])
                    last.then_inc(wstep, 1)

            def aggregate(b, p):
                nc.vector.bn_aggr(mv[:, p, :], bn6[:, p, :, :].rearrange("p c s -> p (c s)")).then_inc(stats, 1)

            def group_spread(b, p):
                dve.wait_ge(mean_mm, b + 1)
                nc.vector.tensor_copy(neg_mean[:, p:p + 1], misc[:, 0:1]).then_inc(wstep, 1)
                nc.vector.tensor_tensor(dmean[:, p:p + 1], misc[:, 0:1], mv[:, p, 0:1], ALU.add).then_inc(wstep, 1)
                dve.wait_ge(wstep, at(b, 4))
                nc.vector.scalar_tensor_tensor(out=spread[:, p:p + 1], in0=dmean[:, p:p + 1],
                                               scalar=dmean[:, p:p + 1], in1=mv[:, p, 1:2],
                                               op0=ALU.mult, op1=ALU.add).then_inc(mean_out, 1)

            def variance_out(b, p):
                dve.wait_ge(var_mm, b + 1)
                nc.vector.tensor_scalar(var_eps[:, p:p + 1], misc[:, 0:1], EPS, None, ALU.add).then_inc(var_out, 1)

            def group_affine(b, p):
                dve.wait_ge(rstd_ready, b + 1)
                r0 = rstd0[:, p:p + 1]
                nc.vector.scalar_tensor_tensor(out=newton[:, p, 0:1], in0=r0, scalar=r0, in1=var_eps[:, p:p + 1],
                                               op0=ALU.mult, op1=ALU.mult).then_inc(wstep, 1)
                dve.wait_ge(wstep, at(b, 5))
                nc.vector.tensor_scalar(newton[:, p, 1:2], newton[:, p, 0:1], -0.5, 1.5,
                                        ALU.mult, ALU.add).then_inc(wstep, 1)
                dve.wait_ge(wstep, at(b, 6))
                nc.vector.scalar_tensor_tensor(out=ga[:, p:p + 1], in0=r0, scalar=newton[:, p, 1:2], in1=gw[:, :],
                                               op0=ALU.mult, op1=ALU.mult).then_inc(wstep, 1)
                dve.wait_ge(wstep, at(b, 7))
                nc.vector.scalar_tensor_tensor(out=gc[:, p:p + 1], in0=neg_mean[:, p:p + 1],
                                               scalar=ga[:, p:p + 1], in1=gb[:, :],
                                               op0=ALU.mult, op1=ALU.add).then_inc(affine, 1)

            def normalise(b, p, first):
                dve.wait_ge(affine, b + 1)
                if not first:
                    dve.wait_ge(h_ready, b)
                nc.vector.tensor_scalar(h[:, :], x_sb[:, p, :], ga[:, p:p + 1], gc[:, p:p + 1],
                                        ALU.mult, ALU.add).then_inc(h_done, 1)

            def tile_max(b, p, n):
                T = TILES * b + n
                dve.wait_ge(qk_done, T + 1)
                nc.vector.tensor_reduce(out=neg_max[:, p, n:n + 1], in_=S[n % 2][:, :], axis=AX.X, op=ALU.max,
                                        negate=True).then_inc(max_step, 1)
                dve.wait_ge(max_step, T + 1)
                if n in (0, 3, 6):
                    dve.wait_ge(c_done, NV * b + n // 3 + 1)
                nc.vector.tensor_scalar(exp_bias[:, p, n:n + 1], neg_max[:, p, n:n + 1], c_tok[:, p, n:n + 1],
                                        c_tok[:, p, n:n + 1], ALU.subtract, ALU.add).then_inc(bias_done, 1)

            def low_parts(b, n):
                T = TILES * b + n
                g = n // GT
                for half in range(2):
                    dve.wait_ge(hi_done, 2 * T + half + 1)
                    ms = slice(half * GT, (half + 1) * GT)
                    nc.vector.scalar_tensor_tensor(out=pT_lo[:, g, ms, n % GT, :], in0=pT[half][:, :, :],
                                                   scalar=P_SCALE, in1=pT_hi[:, g, ms, n % GT, :],
                                                   op0=ALU.mult, op1=ALU.subtract).then_inc(lo_done, 1)

            def reciprocals(b, p, q):
                dve.wait_ge(exp_done, TILES * b + GT * (q + 1))
                nc.vector.tensor_scalar(scaled_sum[:, q, :], row_sum[:, p, q * GT:(q + 1) * GT], P_SCALE, None,
                                        ALU.mult).then_inc(inv_step, 1)
                dve.wait_ge(inv_step, 2 * b + q + 1)
                nc.vector.reciprocal(row_inv[:, q, :], scaled_sum[:, q, :]).then_inc(inv_done, 1)

            def batch(b, p, r, first, last):
                for j in range(TILES):
                    if j == 0 and not last:
                        channel_stats(b + 1, 1 - p, turn(r, p, 1))
                        dve.wait_ge(wstep, at(b + 1, 2))
                    if j < TILES - 1:
                        tile_max(b, p, j + 1)
                    elif not last:
                        tile_max(b + 1, 1 - p, 0)
                    if j == 0 and not last:
                        aggregate(b + 1, 1 - p)
                    if j == 0 and not first:
                        reciprocals(b - 1, 1 - p, 1)
                    if j == 1 and not last:
                        group_spread(b + 1, 1 - p)
                    if j == 2 and not last:
                        variance_out(b + 1, 1 - p)
                    low_parts(b, j)
                    if j == 2 and not last:
                        group_affine(b + 1, 1 - p)
                        normalise(b + 1, 1 - p, False)
                    if j == 5:
                        reciprocals(b, p, 0)

            channel_stats(0, 0, 0)
            dve.wait_ge(wstep, at(0, 2))
            aggregate(0, 0)
            group_spread(0, 0)
            variance_out(0, 0)
            group_affine(0, 0)
            normalise(0, 0, True)
            tile_max(0, 0, 0)
            batch(0, 0, 0, True, False)
            with dve.Fori(0, (B - 2) // 2) as i:
                batch(2 * i + 1, 1, i, False, False)
                batch(2 * i + 2, 0, i + 1, False, False)
            batch(B - 1, 1, B // 2 - 1, False, True)
            reciprocals(B - 1, 1, 1)


_INS = ['x', 'L0_conv_gn_w', 'L0_conv_gn_b', 'L0_conv_wq', 'L0_conv_bq', 'L0_conv_wk', 'L0_conv_bk',
        'L0_conv_wv', 'L0_conv_bv', 'L0_conv_wo', 'L0_conv_bo']
_OUTS = [((8, 128, 32, 32), 'float32')]


def kernel(**inputs):
    import numpy as _np
    import concourse.bacc as _bacc
    from concourse import mybir as _mybir
    from concourse.bass_utils import run_bass_kernel_spmd as _run

    nc = _bacc.Bacc("TRN2", target_bir_lowering=False, num_devices=1)
    arrays, args = {}, []
    for name in _INS:
        a = _np.ascontiguousarray(inputs[name])
        arrays[f"in_{name}_dram"] = a
        args.append(nc.dram_tensor(f"in_{name}_dram", a.shape, _mybir.dt.from_np(a.dtype), kind="ExternalInput").ap())
    for i, (shape, dtype) in enumerate(_OUTS):
        dt = _mybir.dt.from_np(_np.dtype(dtype))
        args.append(nc.dram_tensor(f"out_{i}_dram", shape, dt, kind="ExternalOutput").ap())
    groupnorm_attention_kernel(nc, *args)
    r = _run(nc, [arrays], core_ids=[0])
    return r.results[0]["out_0_dram"]
```

```python
import concourse.bass as bass
from concourse import mybir
from contextlib import ExitStack


def groupnorm_attention_kernel(
    nc: bass.Bass,
    x: bass.AP,
    gn_w: bass.AP,
    gn_b: bass.AP,
    wq: bass.AP,
    bq: bass.AP,
    wk: bass.AP,
    bk: bass.AP,
    wv: bass.AP,
    bv: bass.AP,
    wo: bass.AP,
    bo: bass.AP,
    out: bass.AP,
):
    fp32, fp16 = mybir.dt.float32, mybir.dt.float16
    ALU = mybir.AluOpType
    ACT = mybir.ActivationFunctionType
    AX = mybir.AxisListType

    B, C, HH, WW = x.shape
    N = HH * WW
    GROUPS = 32
    GC = C // GROUPS
    EPS = 1e-5
    SCALE = float(C) ** -0.5
    TILES = N // 128
    GT = 4
    GN = GT * 128
    HALF = 512
    P_SCALE = 4096.0
    VW = C + 1
    V_PARTS = [(0, 3), (3, 3), (6, 2)]
    NV = len(V_PARTS)

    x_d = x.rearrange("b c h w -> b c (h w)")
    out_d = out.rearrange("b c h w -> b c (h w)")

    ctx = ExitStack()
    with ctx:
        def sb(name, shape, dt):
            return ctx.enter_context(nc.sbuf_tensor(name, shape, dt))

        def pb(name, shape, dt):
            return ctx.enter_context(nc.psum_tensor(name, shape, dt))

        def sem(name):
            return ctx.enter_context(nc.semaphore(name))

        wq_sb, wk_sb, wv_sb, wo_sb = (sb(n, [C, C], fp32) for n in ("wq_sb", "wk_sb", "wv_sb", "wo_sb"))
        gw, gb, bq_sb, bk_sb, bv_sb, bo_sb = (
            sb(n, [C, 1], fp32) for n in ("gw", "gb", "bq_sb", "bk_sb", "bv_sb", "bo_sb"))
        ident = sb("ident", [128, 128], fp32)
        neg_mean_mat = sb("neg_mean_mat", [C, C], fp32)
        mean_mat = sb("mean_mat", [C, C], fp32)
        woT = sb("woT", [C, C], fp32)
        wu_hi, wu_lo = sb("wu_hi", [C, C], fp16), sb("wu_lo", [C, C], fp16)
        wvc_hi, wvc_lo = sb("wvc_hi", [C, VW], fp16), sb("wvc_lo", [C, VW], fp16)
        ub = sb("ub", [C, 1], fp32)
        cb = sb("cb", [128, 1], fp32)
        obias = sb("obias", [C, 1], fp32)

        x_sb = sb("x_sb", [C, 2, N], fp32)
        xres = sb("xres", [C, 2, N], fp32)
        bn6 = sb("bn6", [C, 2, 2, 6], fp32)
        mv = sb("mv", [C, 2, 2], fp32)
        neg_mean = sb("neg_mean", [C, 2], fp32)
        dmean = sb("dmean", [C, 2], fp32)
        spread = sb("spread", [C, 2], fp32)
        var_eps = sb("var_eps", [C, 2], fp32)
        ln_var = sb("ln_var", [C, 2], fp32)
        rstd0 = sb("rstd0", [C, 2], fp32)
        newton = sb("newton", [C, 2, 2], fp32)
        ga, gc = sb("ga", [C, 2], fp32), sb("gc", [C, 2], fp32)
        h = sb("h", [C, N], fp32)
        zero = sb("zero", [128, 1], fp32)
        zeros = sb("zeros", [128, 3, C], fp32)
        h_hi, h_lo = sb("h_hi", [C, 2, N], fp16), sb("h_lo", [C, 2, N], fp16)
        u = sb("u", [C, N], fp32)
        v = sb("v", [128, TILES, VW], fp32)
        u_hi, u_lo = sb("u_hi", [C, 2, N], fp16), sb("u_lo", [C, 2, N], fp16)
        v_hi, v_lo = sb("v_hi", [128, 2, TILES, C], fp16), sb("v_lo", [128, 2, TILES, C], fp16)
        c_tok = sb("c_tok", [128, 2, TILES], fp32)

        neg_max = sb("neg_max", [128, 2, TILES], fp32)
        exp_bias = sb("exp_bias", [128, 2, TILES], fp32)
        row_sum = sb("row_sum", [128, 2, TILES], fp32)
        scaled_sum = sb("scaled_sum", [128, 2, GT], fp32)
        row_inv = sb("row_inv", [128, 2, GT], fp32)
        probs = sb("probs", [128, 2, N], fp32)
        pT_hi = sb("pT_hi", [128, 2, TILES, GT, 128], fp16)
        pT_lo = sb("pT_lo", [128, 2, TILES, GT, 128], fp16)
        inv_rows = sb("inv_rows", [C, 2, 128, GT], fp32)
        av = sb("av", [C, 2, GN], fp32)
        attn = sb("attn", [C, 2, GN], fp32)
        y = sb("y", [C, 2, GN], fp32)

        inv_line = nc.dram_tensor("inv_line", [2, 128, GT], fp32).ap()

        S = [pb(f"S{i}", [128, N], fp32) for i in range(2)]
        pT = [pb(f"pT{i}", [128, GT, 128], fp32) for i in range(2)]
        O = pb("O", [C, GN], fp32)
        misc = pb("misc", [128, HALF], fp32)

        wqk_in, wvo_in, bias_in, gn_in = sem("wqk_in"), sem("wvo_in"), sem("bias_in"), sem("gn_in")
        x0_in = sem("x0_in")
        x_in = [sem(f"x_in{p}") for p in range(2)]
        y_out = [sem(f"y_out{q}") for q in range(2)]
        pool_step = sem("pool_step")
        consts = sem("consts")
        a_mm, small_mm, woT_mm, b_mm = (
            sem(n) for n in ("a_mm", "small_mm", "woT_mm", "b_mm"))
        a_hi, cw_hi, b_hi = sem("a_hi"), sem("cw_hi"), sem("b_hi")
        ub_cb = sem("ub_cb")
        woT_out = sem("woT_out")
        ob_out = sem("ob_out")
        w_lo = sem("w_lo")
        h0_part, h0_hi = sem("h0_part"), sem("h0_hi")
        u0_mm = sem("u0_mm")
        u0_hi = sem("u0_hi")
        u0_done = sem("u0_done")
        tail_step = sem("tail_step")
        wstep = sem("wstep")
        stats = sem("stats")
        mean_mm, var_mm = sem("mean_mm"), sem("var_mm")
        mean_out = sem("mean_out")
        var_out = sem("var_out")
        ln_step = sem("ln_step")
        rstd_ready = sem("rstd_ready")
        affine = sem("affine")
        h_done = sem("h_done")
        h_step = sem("h_step")
        h_ready = sem("h_ready")
        xres_done = sem("xres_done")
        u_mm, v_mm = sem("u_mm"), sem("v_mm")
        u_out, v_out = sem("u_out"), sem("v_out")
        u_step, v_step = sem("u_step"), sem("v_step")
        u_done, v_done = sem("u_done"), sem("v_done")
        c_done = sem("c_done")
        qk_done = sem("qk_done")
        max_step = sem("max_step")
        bias_done = sem("bias_done")
        exp_done = sem("exp_done")
        tr_done = sem("tr_done")
        hi_done = sem("hi_done")
        lo_done = sem("lo_done")
        av_done = sem("av_done")
        last_av = sem("last_av")
        inv_step = sem("inv_step")
        inv_done = sem("inv_done")
        line_out = [sem(f"line_out{q}") for q in range(2)]
        rows_in = [sem(f"rows_in{q}") for q in range(2)]
        av_out = sem("av_out")
        attn_done = sem("attn_done")
        y_done = sem("y_done")

        block = ctx.enter_context(nc.Block())

        UB, CW, CB, OB = (O[:, i:i + 1] for i in range(4))
        WOT, BM = S[1][:, 0:C], S[1][:, HALF:HALF + C]
        U0_PARTS = ((slice(0, 128), pT[0][:, 0, :]), (slice(128, HALF), misc[:, 128:HALF]))
        WARM = (5, 2)
        LAST = (slice(0, GT // 2), slice(GT // 2, GT))

        def by_tile(a):
            return a.rearrange("c (t n) -> c t n", t=GT)

        def inverses(q):
            return inv_rows[:, q, :, :].rearrange("c n t -> c t n")

        def turn(r, p, d):
            return r + (p + d) // 2

        def group_of(b, j):
            past = j - GT
            d = -1 if past < 0 else 0
            q = (past // GT) % 2
            return q, d, 2 * (b + d) + q, past % GT

        @block.sync
        def _(eng):
            def load_x(b, p):
                eng.dma_start(x_sb[:, p, :], x_d[b, :, :]).then_inc(x_in[p], 16)

            def store(b, q):
                eng.wait_ge(y_done, 2 * b + q + 1)
                eng.dma_start(out_d[b, :, q * GN:(q + 1) * GN], y[:, q, :]).then_inc(y_out[q], 16)

            def spread_inverse(b, q, first):
                eng.wait_ge(inv_done, 2 * b + q + 1)
                if not first:
                    eng.wait_ge(rows_in[q], 16 * b)
                eng.dma_start(inv_line[q, :, :], row_inv[:, q, :]).then_inc(line_out[q], 16)
                eng.wait_ge(line_out[q], 16 * b + 16)
                if not first:
                    eng.wait_ge(attn_done, 2 * b + q - 1)
                eng.dma_start(inv_rows[:, q, :, :].rearrange("c n t -> c (n t)"),
                              inv_line[q, :, :].rearrange("n t -> (n t)").partition_broadcast(C)
                              ).then_inc(rows_in[q], 16)

            def batch(b, p, load, first=False, second=False):
                if not first:
                    spread_inverse(b - 1, 1, second)
                    store(b - 1, 0)
                spread_inverse(b, 0, first)
                if not first:
                    store(b - 1, 1)
                if load:
                    eng.wait_ge(xres_done, b + 2)
                    load_x(b + 3, 1 - p)

            for half, landed in enumerate((x0_in, x_in[0])):
                cols = slice(half * HALF, (half + 1) * HALF)
                eng.dma_start(x_sb[:, 0, cols], x_d[0, :, cols]).then_inc(landed, 16)
            for dst, src in ((gw, gn_w), (gb, gn_b)):
                eng.dma_start(dst[:, :], src.rearrange("(c one) -> c one", one=1)).then_inc(gn_in, 16)
            for dst, src in ((wo_sb, wo), (wv_sb, wv)):
                eng.dma_start(dst[:, :], src).then_inc(wvo_in, 16)
            for dst, src in ((bq_sb, bq), (bk_sb, bk), (bv_sb, bv), (bo_sb, bo)):
                eng.dma_start(dst[:, :], src.rearrange("(c one) -> c one", one=1)).then_inc(bias_in, 16)
            load_x(1, 1)
            eng.wait_ge(xres_done, 1)
            load_x(2, 0)
            batch(0, 0, True, True)
            batch(1, 1, True, False, True)
            batch(2, 0, True)
            with eng.Fori(1, (B - 4) // 2) as i:
                batch(2 * i + 1, 1, True)
                batch(2 * i + 2, 0, True)
            for b in range(B - 3, B):
                batch(b, b % 2, False)
            spread_inverse(B - 1, 1, False)
            store(B - 1, 0)
            for half in range(2):
                eng.wait_ge(y_done, 2 * B + half)
                cols = slice(half * GN // 2, (half + 1) * GN // 2)
                eng.dma_start(out_d[B - 1, :, GN + cols.start:GN + cols.stop],
                              y[:, 1, cols]).then_inc(y_out[1], 16)
            for q in range(2):
                eng.wait_ge(line_out[q], 16 * B)
            for q in range(2):
                eng.wait_ge(y_out[q], 16 * (B + q))

        @block.gpsimd
        def _(eng):
            nc.gpsimd.memset(ident[:, :], 0.0).then_inc(pool_step, 1)
            nc.gpsimd.memset(neg_mean_mat[:, :], -1.0 / GC).then_inc(pool_step, 1)
            nc.gpsimd.memset(mean_mat[:, :], 1.0 / GC).then_inc(pool_step, 1)
            nc.gpsimd.memset(zero[:, :], 0.0).then_inc(pool_step, 1)
            nc.gpsimd.memset(zeros[:, :, :], 0.0).then_inc(pool_step, 1)
            eng.wait_ge(pool_step, 5)
            nc.gpsimd.affine_select(out=ident[:, :], in_=ident[:, :], compare_op=ALU.not_equal, fill=1.0,
                                    base=0, pattern=[[-1, 128]], channel_multiplier=1).then_inc(consts, 1)
            for m in (neg_mean_mat, mean_mat):
                nc.gpsimd.affine_select(out=m[:, :], in_=m[:, :], compare_op=ALU.is_ge, fill=0.0,
                                        base=0, pattern=[[-GC, GROUPS], [0, GC]],
                                        channel_multiplier=1).then_inc(pool_step, 1)
            eng.wait_ge(pool_step, 7)
            for m in (neg_mean_mat, mean_mat):
                nc.gpsimd.affine_select(out=m[:, :], in_=m[:, :], compare_op=ALU.is_ge, fill=0.0,
                                        base=GC - 1, pattern=[[GC, GROUPS], [0, GC]],
                                        channel_multiplier=-1).then_inc(consts, 1)

            def h_parts(b, p, first):
                if not first:
                    eng.wait_ge(qk_done, (b - 1) * TILES)
                for half in range(2):
                    eng.wait_ge(h_done, 2 * b - 1 + half)
                    cols = slice(half * HALF, (half + 1) * HALF)
                    nc.gpsimd.tensor_tensor(h_hi[:, p, cols], h[:, cols], zero[:, :].to_broadcast([C, HALF]),
                                            ALU.add).then_inc(h_step, 1)
                    eng.wait_ge(h_step, 2 * b - 1 + half)
                    nc.gpsimd.tensor_tensor(h_lo[:, p, cols], h[:, cols], h_hi[:, p, cols],
                                            ALU.subtract).then_inc(h_ready, 1)

            def u_parts(b, p, half):
                cols = slice(half * HALF, (half + 1) * HALF)
                eng.wait_ge(u_out, 2 * b + half)
                nc.gpsimd.tensor_tensor(u_hi[:, p, cols], u[:, cols], zero[:, :].to_broadcast([C, HALF]),
                                        ALU.add).then_inc(u_step, 1)
                eng.wait_ge(u_step, 2 * b + half)
                nc.gpsimd.tensor_tensor(u_lo[:, p, cols], u[:, cols], u_hi[:, p, cols],
                                        ALU.subtract).then_inc(u_done, 1)

            def v_parts(b, p, part, first):
                t0, n = V_PARTS[part]
                eng.wait_ge(v_out, NV * b + part + 1)
                nc.gpsimd.tensor_tensor(c_tok[:, p, t0:t0 + n], v[:, t0:t0 + n, C],
                                        cb[:, :].to_broadcast([128, n]), ALU.add).then_inc(c_done, 1)
                if part == 0 and not first:
                    eng.wait_ge(av_done, TILES * (b - 1))
                nc.gpsimd.tensor_tensor(v_hi[:, p, t0:t0 + n, :], v[:, t0:t0 + n, 0:C],
                                        zeros[:, 0:n, :], ALU.add).then_inc(v_step, 1)
                eng.wait_ge(v_step, NV * b + part + 1)
                nc.gpsimd.tensor_tensor(v_lo[:, p, t0:t0 + n, :], v[:, t0:t0 + n, 0:C],
                                        v_hi[:, p, t0:t0 + n, :], ALU.subtract).then_inc(v_done, 1)

            def residual(b, p):
                nc.gpsimd.tensor_tensor(xres[:, p, :], x_sb[:, p, :], obias[:, :].to_broadcast([C, N]),
                                        ALU.add).then_inc(xres_done, 1)

            def result(b, p, q, first):
                g = 2 * b + q
                eng.wait_ge(rows_in[q], 16 * b + 16)
                eng.wait_ge(av_out, g + 1)
                nc.gpsimd.tensor_tensor(by_tile(attn[:, q, :]), by_tile(av[:, q, :]), inverses(q),
                                        ALU.mult).then_inc(attn_done, 1)
                eng.wait_ge(xres_done, b + 1)
                eng.wait_ge(attn_done, g + 1)
                if not first:
                    eng.wait_ge(y_out[q], 16 * b)
                nc.gpsimd.tensor_tensor(y[:, q, :], attn[:, q, :], xres[:, p, q * GN:(q + 1) * GN],
                                        ALU.add).then_inc(y_done, 1)

            def batch(b, p, after_first, after_second, last):
                u_parts(b, p, 1)
                v_parts(b, p, 1, False)
                if after_first:
                    result(b - 1, 1 - p, 0, not after_second)
                if not last:
                    h_parts(b + 1, 1 - p, not after_first)
                v_parts(b, p, 2, False)
                if not last:
                    u_parts(b + 1, 1 - p, 0)
                    v_parts(b + 1, 1 - p, 0, not after_first)
                if after_first:
                    result(b - 1, 1 - p, 1, not after_second)
                if not last:
                    if after_first:
                        eng.wait_ge(y_done, 2 * b)
                    residual(b + 1, 1 - p)

            v_parts(0, 0, 0, True)
            eng.wait_ge(ob_out, 1)
            residual(0, 0)
            batch(0, 0, False, False, False)
            batch(1, 1, True, False, False)
            batch(2, 0, True, True, False)
            with eng.Fori(1, (B - 2) // 2) as i:
                batch(2 * i + 1, 1, True, True, False)
                batch(2 * i + 2, 0, True, True, False)
            batch(B - 1, 1, True, True, True)
            result(B - 1, 1, 0, False)

        @block.tensor
        def _(pe):
            def split_product(o, l_hi, l_lo, r_hi, r_lo):
                nc.tensor.matmul(o, l_hi, r_hi, start=True, stop=False)
                nc.tensor.matmul(o, l_hi, r_lo, start=False, stop=False)
                return nc.tensor.matmul(o, l_lo, r_hi, start=False, stop=True)

            def group_mean(b, p):
                pe.wait_ge(stats, b + 1)
                nc.tensor.matmul(misc[:, 0:1], neg_mean_mat[:, :], mv[:, p, 0:1],
                                 start=True, stop=True).then_inc(mean_mm, 1)

            def group_var(b, p):
                pe.wait_ge(mean_out, b + 1)
                nc.tensor.matmul(misc[:, 0:1], mean_mat[:, :], spread[:, p:p + 1],
                                 start=True, stop=True).then_inc(var_mm, 1)

            def project_u(b, p, half):
                pe.wait_ge(h_ready, 2 * b + half + 1)
                cols = slice(half * HALF, (half + 1) * HALF)
                split_product(misc[:, :], wu_hi[:, :], wu_lo[:, :], h_hi[:, p, cols],
                              h_lo[:, p, cols]).then_inc(u_mm, 1)

            def project_v(b, p, part, bank=misc):
                t0, n = V_PARTS[part]
                for k in range(n):
                    tok = slice((t0 + k) * 128, (t0 + k + 1) * 128)
                    last = split_product(bank[:, k * VW:(k + 1) * VW], h_hi[:, p, tok], h_lo[:, p, tok],
                                         wvc_hi[:, :], wvc_lo[:, :])
                last.then_inc(v_mm, 1)

            def logits(b, p, n, first):
                T = TILES * b + n
                if n == 0:
                    pe.wait_ge(h_ready, 2 * b + 2)
                    if first:
                        pe.wait_ge(u0_done, 1)
                    else:
                        pe.wait_ge(u_done, 2 * b + 1)
                if n == 1 and first:
                    pe.wait_ge(u_done, 1)
                if n == GT:
                    pe.wait_ge(u_done, 2 * b + 2)
                if not first:
                    pe.wait_ge(exp_done, T - 1)
                s, q_hi, q_lo = S[n % 2], u_hi[:, p, n * 128:(n + 1) * 128], u_lo[:, p, n * 128:(n + 1) * 128]
                halves = [slice(c * HALF, (c + 1) * HALF) for c in range(N // HALF)]
                for c in halves:
                    nc.tensor.matmul(s[:, c], q_hi, h_hi[:, p, c], start=True, stop=False)
                for c in halves:
                    nc.tensor.matmul(s[:, c], q_hi, h_lo[:, p, c], start=False, stop=False)
                for c in halves:
                    last = nc.tensor.matmul(s[:, c], q_lo, h_hi[:, p, c], start=False, stop=True)
                last.then_inc(qk_done, 1)

            def values(b, j, p, first_group):
                q, d, g, k = group_of(b, j)
                pv = (p + d) % 2
                if q == 0 and k != 2:
                    pe.wait_ge(v_done, NV * (b + d) + (1, 2, 2, 3)[k])
                if k == 2:
                    pe.wait_ge(lo_done, 2 * GT * (g + 1))
                if k == 0:
                    pe.wait_ge(lo_done, 2 * GT * (g + 1) - 1)
                    if not first_group:
                        pe.wait_ge(av_out, g)
                for m in (2 * k, 2 * k + 1):
                    vh, vl = v_hi[:, pv, m, 0:C], v_lo[:, pv, m, 0:C]
                    ph = pT_hi[:, q, m, :, :].rearrange("p t n -> p (t n)")
                    pl = pT_lo[:, q, m, :, :].rearrange("p t n -> p (t n)")
                    nc.tensor.matmul(O[:, :], vh, ph, start=(m == 0), stop=False)
                    nc.tensor.matmul(O[:, :], vh, pl, start=False, stop=False)
                    last = nc.tensor.matmul(O[:, :], vl, ph, start=False, stop=(m == TILES - 1))
                last.then_inc(av_done, 1)

            def last_values(half, key_tiles):
                bank = (misc, O)[half]
                if key_tiles[0] == 0 and half == 0:
                    pe.wait_ge(v_done, NV * B)
                if key_tiles[0] == 0:
                    pe.wait_ge(lo_done, 2 * (TILES * B - GT // 2 * (1 - half)))
                if half == 1:
                    pe.wait_ge(av_out, 2 * B - 1)
                for m in key_tiles:
                    vh, vl = v_hi[:, 1, m, 0:C], v_lo[:, 1, m, 0:C]
                    ph, pl = (a[:, 1, m, LAST[half], :].rearrange("p t n -> p (t n)") for a in (pT_hi, pT_lo))
                    o = bank[:, 0:GN // 2]
                    nc.tensor.matmul(o, vh, ph, start=(m == 0), stop=False)
                    nc.tensor.matmul(o, vh, pl, start=False, stop=False)
                    done = nc.tensor.matmul(o, vl, ph, start=False, stop=(m == TILES - 1))
                if key_tiles[-1] == TILES - 1:
                    done.then_inc(last_av, 1)

            def transposes(b, n, first):
                T = TILES * b + n
                pe.wait_ge(exp_done, T + 1)
                for half in range(2):
                    if not first:
                        pe.wait_ge(lo_done, 2 * T - 1 + half)
                    for t in range(GT):
                        m = half * GT + t
                        last = nc.tensor.transpose(pT[half][:, t, :], probs[:, n % 2, m * 128:(m + 1) * 128],
                                                   ident[:, :])
                    last.then_inc(tr_done, 1)

            def batch(b, p, first, last):
                np = 1 - p
                for j in range(TILES):
                    if j < TILES - 1:
                        logits(b, p, j + 1, first and j == 0)
                    elif not last:
                        logits(b + 1, np, 0, False)
                    if j == 1:
                        pe.wait_ge(u_out, 2 * b + 1)
                        project_v(b, p, 1)
                    if j == 5 and not last:
                        pe.wait_ge(v_out, NV * b + 3)
                        project_u(b + 1, np, 0)
                    if j == 6 and not last:
                        pe.wait_ge(u_out, 2 * b + 2)
                        project_v(b + 1, np, 0)
                    if not first or j >= GT:
                        values(b, j, p, first and j == GT)
                    if last and j == TILES - 1:
                        last_values(0, (0, 1))
                    if j == 0:
                        if not first:
                            pe.wait_ge(v_out, NV * b + 1)
                        project_u(b, p, 1)
                    if j == 4:
                        if last:
                            pe.wait_ge(v_out, NV * b + 2)
                        else:
                            pe.wait_ge(var_out, b + 2)
                        project_v(b, p, 2)
                    transposes(b, j, first and j == 0)
                    if last and j == TILES - 1:
                        last_values(0, range(2, TILES))
                    if j == 1 and not last:
                        pe.wait_ge(v_out, NV * b + 2)
                        group_mean(b + 1, np)
                    if j == 2 and not last:
                        group_var(b + 1, np)

            def warm_up(count):
                for t in range(count):
                    nc.tensor.transpose(pT[1][:, t % GT, :], ident[:, :], ident[:, :])

            pe.wait_ge(wqk_in, 32)
            nc.tensor.matmul(S[0][:, 0:C], wq_sb[:, :], wk_sb[:, :], start=True, stop=True).then_inc(a_mm, 1)
            pe.wait_ge(consts, 3)
            group_mean(0, 0)
            pe.wait_ge(wvo_in, 32)
            nc.tensor.transpose(WOT, wo_sb[:, :], ident[:, :]).then_inc(woT_mm, 1)
            group_var(0, 0)
            pe.wait_ge(woT_out, 1)
            nc.tensor.matmul(BM, wv_sb[:, :], woT[:, :], start=True, stop=True).then_inc(b_mm, 1)
            warm_up(WARM[0])
            pe.wait_ge(bias_in, 64)
            nc.tensor.matmul(UB, wk_sb[:, :], bq_sb[:, :], start=True, stop=True)
            nc.tensor.matmul(CW, wq_sb[:, :], bk_sb[:, :], start=True, stop=True)
            nc.tensor.matmul(CB, bq_sb[:, 0:1].to_broadcast([C, 128]), bk_sb[:, :],
                             start=True, stop=True)
            nc.tensor.matmul(OB, woT[:, :], bv_sb[:, :], start=True, stop=True).then_inc(small_mm, 1)
            warm_up(WARM[1])
            pe.wait_ge(w_lo, 1)
            pe.wait_ge(var_out, 1)
            pe.wait_ge(h_ready, 1)
            for (cols, bank), made in zip(U0_PARTS, (u0_mm, u_mm)):
                split_product(bank, wu_hi[:, :], wu_lo[:, :], h_hi[:, 0, cols],
                              h_lo[:, 0, cols]).then_inc(made, 1)
            logits(0, 0, 0, True)
            pe.wait_ge(w_lo, 3)
            project_v(0, 0, 0, O)
            batch(0, 0, True, False)
            with pe.Fori(0, (B - 2) // 2) as i:
                batch(2 * i + 1, 1, False, False)
                batch(2 * i + 2, 0, False, False)
            batch(B - 1, 1, False, True)
            last_values(1, range(TILES))

        @block.scalar
        def _(act):
            for dst, src in ((wq_sb, wq), (wk_sb, wk)):
                act.dma_start(dst[:, :], src).then_inc(wqk_in, 16)
            def copy_u(b, half, first):
                act.wait_ge(u_mm, 2 * b + half + 1)
                if not first:
                    act.wait_ge(u_done, 2 * b + half - 1)
                nc.scalar.activation(u[:, half * HALF:(half + 1) * HALF], misc[:, :], ACT.Identity,
                                     bias=ub[:, :]).then_inc(u_out, 1)

            def copy_v(b, part, first, bank=misc):
                t0, n = V_PARTS[part]
                act.wait_ge(v_mm, NV * b + part + 1)
                if not first:
                    act.wait_ge(v_done, NV * (b - 1) + part + 1)
                nc.scalar.copy(v[:, t0:t0 + n, :].rearrange("p t c -> p (t c)"),
                               bank[:, 0:n * VW]).then_inc(v_out, 1)

            def copy_values(b, q, first):
                act.wait_ge(av_done, GT * (2 * b + q + 1))
                if not first:
                    act.wait_ge(attn_done, 2 * b + q - 1)
                nc.scalar.copy(av[:, q, :], O[:, :]).then_inc(av_out, 1)

            def inverse_deviation(b, p):
                act.wait_ge(var_out, b + 1)
                nc.scalar.activation(ln_var[:, p:p + 1], var_eps[:, p:p + 1], ACT.Ln).then_inc(ln_step, 1)
                act.wait_ge(ln_step, b + 1)
                nc.scalar.activation(rstd0[:, p:p + 1], ln_var[:, p:p + 1], ACT.Exp,
                                     scale=-0.5).then_inc(rstd_ready, 1)

            def exponentials(b, p, n, first):
                T = TILES * b + n
                act.wait_ge(bias_done, T + 1)
                if not first:
                    act.wait_ge(tr_done, 2 * T - 2)
                nc.scalar.activation(probs[:, n % 2, :], S[n % 2][:, :], ACT.Exp, bias=exp_bias[:, p, n:n + 1],
                                     accum_out=row_sum[:, p, n:n + 1]).then_inc(exp_done, 1)

            def high_parts(b, p, n, free):
                T = TILES * b + n
                g = n // GT
                for half in range(2):
                    act.wait_ge(tr_done, 2 * T + half + 1)
                    if n % GT == 0 and half == 0 and free:
                        act.wait_ge(av_done, GT * (2 * b + g - 1))
                    nc.scalar.activation(pT_hi[:, g, half * GT:(half + 1) * GT, n % GT, :], pT[half][:, :, :],
                                         ACT.Copy, scale=P_SCALE).then_inc(hi_done, 1)

            def batch(b, p, first, second, last):
                for j in range(TILES):
                    if j == 0:
                        copy_u(b, 1, first)
                    if j == 1:
                        copy_v(b, 1, first)
                    if j == 3 and not first:
                        copy_values(b - 1, 1, second)
                    if j == 4:
                        copy_v(b, 2, first)
                    if j == 5 and not last:
                        copy_u(b + 1, 0, False)
                    if j == 6 and not last:
                        copy_v(b + 1, 0, False)
                    if j == 7:
                        copy_values(b, 0, first)
                    high_parts(b, p, j, not first)
                    if j < TILES - 1:
                        exponentials(b, p, j + 1, first and j == 0)
                        if j == 2 and not last:
                            inverse_deviation(b + 1, 1 - p)
                    elif not last:
                        exponentials(b + 1, 1 - p, 0, False)

            nc.scalar.preload_act_table_set("natural_log_exp_and_others")
            act.wait_ge(a_mm, 1)
            nc.scalar.activation(wu_hi[:, :], S[0][:, 0:C], ACT.Copy, scale=SCALE).then_inc(a_hi, 1)
            act.wait_ge(woT_mm, 1)
            nc.scalar.copy(woT[:, :], WOT).then_inc(woT_out, 1)
            inverse_deviation(0, 0)
            act.wait_ge(b_mm, 1)
            nc.scalar.copy(wvc_hi[:, 0:C], BM).then_inc(b_hi, 1)
            for half in range(2):
                act.wait_ge(h0_part, half + 1)
                nc.scalar.copy(h_hi[:, 0, half * HALF:(half + 1) * HALF],
                               h[:, half * HALF:(half + 1) * HALF]).then_inc(h0_hi, 1)
            act.wait_ge(small_mm, 1)
            nc.scalar.activation(wvc_hi[:, C:C + 1], CW, ACT.Copy, scale=SCALE).then_inc(cw_hi, 1)
            nc.scalar.activation(ub[:, :], UB, ACT.Copy, scale=SCALE).then_inc(ub_cb, 1)
            nc.scalar.activation(cb[:, :], CB, ACT.Copy, scale=SCALE).then_inc(ub_cb, 1)
            nc.scalar.activation(obias[:, :], OB, ACT.Identity, bias=bo_sb[:, :]).then_inc(ob_out, 1)
            act.wait_ge(ub_cb, 2)
            for (cols, bank), made in zip(U0_PARTS, (u0_mm, u_mm)):
                act.wait_ge(made, 1)
                nc.scalar.activation(u_hi[:, 0, cols], bank, ACT.Identity, bias=ub[:, :]).then_inc(u0_hi, 1)
            copy_v(0, 0, True, O)
            exponentials(0, 0, 0, True)
            batch(0, 0, True, False, False)
            batch(1, 1, False, True, False)
            batch(2, 0, False, False, False)
            with act.Fori(1, (B - 2) // 2) as i:
                batch(2 * i + 1, 1, False, False, False)
                batch(2 * i + 2, 0, False, False, False)
            batch(B - 1, 1, False, False, True)

        @block.vector
        def _(dve):
            STAT_STEPS, MEAN_STEPS, VAR_STEPS = 2, 2, 3

            def at(b, k):
                return (STAT_STEPS + MEAN_STEPS + VAR_STEPS) * b + k

            def channel_stats(b, p, r, halves=(0, 1)):
                dve.wait_ge(x_in[p], 16 * r + 16)
                for c in halves:
                    last = nc.vector.bn_stats(bn6[:, p, c, :], x_sb[:, p, c * HALF:(c + 1) * HALF])
                    last.then_inc(wstep, 1)

            def aggregate(b, p):
                nc.vector.bn_aggr(mv[:, p, :], bn6[:, p, :, :].rearrange("p c s -> p (c s)")).then_inc(stats, 1)

            def group_spread(b, p):
                dve.wait_ge(mean_mm, b + 1)
                nc.vector.tensor_copy(neg_mean[:, p:p + 1], misc[:, 0:1]).then_inc(wstep, 1)
                nc.vector.tensor_tensor(dmean[:, p:p + 1], misc[:, 0:1], mv[:, p, 0:1], ALU.add).then_inc(wstep, 1)
                dve.wait_ge(wstep, at(b, 4))
                nc.vector.scalar_tensor_tensor(out=spread[:, p:p + 1], in0=dmean[:, p:p + 1],
                                               scalar=dmean[:, p:p + 1], in1=mv[:, p, 1:2],
                                               op0=ALU.mult, op1=ALU.add).then_inc(mean_out, 1)

            def variance_out(b, p):
                dve.wait_ge(var_mm, b + 1)
                nc.vector.tensor_scalar(var_eps[:, p:p + 1], misc[:, 0:1], EPS, None, ALU.add).then_inc(var_out, 1)

            def group_affine(b, p):
                dve.wait_ge(rstd_ready, b + 1)
                r0 = rstd0[:, p:p + 1]
                nc.vector.scalar_tensor_tensor(out=newton[:, p, 0:1], in0=r0, scalar=r0, in1=var_eps[:, p:p + 1],
                                               op0=ALU.mult, op1=ALU.mult).then_inc(wstep, 1)
                dve.wait_ge(wstep, at(b, 5))
                nc.vector.tensor_scalar(newton[:, p, 1:2], newton[:, p, 0:1], -0.5, 1.5,
                                        ALU.mult, ALU.add).then_inc(wstep, 1)
                dve.wait_ge(wstep, at(b, 6))
                nc.vector.scalar_tensor_tensor(out=ga[:, p:p + 1], in0=r0, scalar=newton[:, p, 1:2], in1=gw[:, :],
                                               op0=ALU.mult, op1=ALU.mult).then_inc(wstep, 1)
                dve.wait_ge(wstep, at(b, 7))
                nc.vector.scalar_tensor_tensor(out=gc[:, p:p + 1], in0=neg_mean[:, p:p + 1],
                                               scalar=ga[:, p:p + 1], in1=gb[:, :],
                                               op0=ALU.mult, op1=ALU.add).then_inc(affine, 1)

            def normalise(b, p, half):
                if half == 0:
                    dve.wait_ge(affine, b + 1)
                    dve.wait_ge(h_ready, 2 * b)
                cols = slice(half * HALF, (half + 1) * HALF)
                nc.vector.tensor_scalar(h[:, cols], x_sb[:, p, cols], ga[:, p:p + 1], gc[:, p:p + 1],
                                        ALU.mult, ALU.add).then_inc(h_done, 1)

            def tile_max(b, p, n):
                T = TILES * b + n
                dve.wait_ge(qk_done, T + 1)
                nc.vector.tensor_reduce(out=neg_max[:, p, n:n + 1], in_=S[n % 2][:, :], axis=AX.X, op=ALU.max,
                                        negate=True).then_inc(max_step, 1)
                dve.wait_ge(max_step, T + 1)
                if n in (0, 3, 6):
                    dve.wait_ge(c_done, NV * b + n // 3 + 1)
                nc.vector.tensor_scalar(exp_bias[:, p, n:n + 1], neg_max[:, p, n:n + 1], c_tok[:, p, n:n + 1],
                                        c_tok[:, p, n:n + 1], ALU.subtract, ALU.add).then_inc(bias_done, 1)

            def low_parts(b, n, halves=(0, 1)):
                T = TILES * b + n
                g = n // GT
                for half in halves:
                    dve.wait_ge(hi_done, 2 * T + half + 1)
                    ms = slice(half * GT, (half + 1) * GT)
                    nc.vector.scalar_tensor_tensor(out=pT_lo[:, g, ms, n % GT, :], in0=pT[half][:, :, :],
                                                   scalar=P_SCALE, in1=pT_hi[:, g, ms, n % GT, :],
                                                   op0=ALU.mult, op1=ALU.subtract).then_inc(lo_done, 1)

            def reciprocals(b, p, q, first):
                dve.wait_ge(exp_done, TILES * b + GT * (q + 1))
                if not first:
                    dve.wait_ge(line_out[q], 16 * b)
                nc.vector.tensor_scalar(scaled_sum[:, q, :], row_sum[:, p, q * GT:(q + 1) * GT], P_SCALE, None,
                                        ALU.mult).then_inc(inv_step, 1)
                dve.wait_ge(inv_step, 2 * b + q + 1)
                nc.vector.reciprocal(row_inv[:, q, :], scaled_sum[:, q, :]).then_inc(inv_done, 1)

            def batch(b, p, r, first, second, last):
                for j in range(TILES):
                    if j == 0 and not (first or last):
                        channel_stats(b + 1, 1 - p, turn(r, p, 1))
                        dve.wait_ge(wstep, at(b + 1, 2))
                    if j < TILES - 1:
                        tile_max(b, p, j + 1)
                    elif not last:
                        tile_max(b + 1, 1 - p, 0)
                    else:
                        reciprocals(b, p, 1, False)
                    if j == 0 and not (first or last):
                        aggregate(b + 1, 1 - p)
                    if j == 0 and not first:
                        reciprocals(b - 1, 1 - p, 1, second)
                    if j == 1 and not last:
                        group_spread(b + 1, 1 - p)
                    if j == 4 and not last:
                        normalise(b + 1, 1 - p, 1)
                    if j == 2 and not last:
                        variance_out(b + 1, 1 - p)
                    if j == 3 and not last:
                        low_parts(b, j, (0,))
                        group_affine(b + 1, 1 - p)
                        normalise(b + 1, 1 - p, 0)
                        low_parts(b, j, (1,))
                    else:
                        low_parts(b, j)
                    if j == 5:
                        reciprocals(b, p, 0, first)

            dve.wait_ge(x0_in, 16)
            nc.vector.bn_stats(bn6[:, 0, 0, :], x_sb[:, 0, 0:HALF]).then_inc(wstep, 1)
            channel_stats(0, 0, 0, (1,))
            dve.wait_ge(wstep, at(0, 2))
            aggregate(0, 0)
            group_spread(0, 0)
            dve.wait_ge(a_hi, 1)
            nc.vector.scalar_tensor_tensor(out=wu_lo[:, :], in0=S[0][:, 0:C], scalar=SCALE, in1=wu_hi[:, :],
                                           op0=ALU.mult, op1=ALU.subtract).then_inc(w_lo, 1)
            variance_out(0, 0)
            dve.wait_ge(gn_in, 32)
            group_affine(0, 0)
            dve.wait_ge(affine, 1)
            halves = [slice(half * HALF, (half + 1) * HALF) for half in range(2)]
            for c in halves:
                nc.vector.tensor_scalar(h[:, c], x_sb[:, 0, c], ga[:, 0:1], gc[:, 0:1],
                                        ALU.mult, ALU.add).then_inc(h0_part, 1)
            for half in range(2):
                dve.wait_ge(h0_hi, half + 1)
                nc.vector.tensor_tensor(h_lo[:, 0, halves[half]], h[:, halves[half]], h_hi[:, 0, halves[half]],
                                        ALU.subtract).then_inc(h_ready, 1)
            channel_stats(1, 1, 0, (0,))
            dve.wait_ge(ub_cb, 2)
            for i, ((cols, bank), made) in enumerate(zip(U0_PARTS, (u0_done, u_done))):
                dve.wait_ge(u0_hi, i + 1)
                nc.vector.scalar_tensor_tensor(out=u_lo[:, 0, cols], in0=bank, scalar=ub[:, :],
                                               in1=u_hi[:, 0, cols], op0=ALU.add,
                                               op1=ALU.subtract).then_inc(made, 1)
                if i == 0:
                    dve.wait_ge(b_hi, 1)
                    nc.vector.tensor_tensor(wvc_lo[:, 0:C], BM, wvc_hi[:, 0:C], ALU.subtract).then_inc(w_lo, 1)
                    dve.wait_ge(cw_hi, 1)
                    dve.wait_ge(ob_out, 1)
                    nc.vector.scalar_tensor_tensor(out=wvc_lo[:, C:C + 1], in0=CW, scalar=SCALE,
                                                   in1=wvc_hi[:, C:C + 1], op0=ALU.mult,
                                                   op1=ALU.subtract).then_inc(w_lo, 1)
                    channel_stats(1, 1, 0, (1,))
            dve.wait_ge(wstep, at(1, 2))
            aggregate(1, 1)
            tile_max(0, 0, 0)
            batch(0, 0, 0, True, False, False)
            batch(1, 1, 0, False, True, False)
            batch(2, 0, 1, False, False, False)
            with dve.Fori(1, (B - 2) // 2) as i:
                batch(2 * i + 1, 1, i, False, False, False)
                batch(2 * i + 2, 0, i + 1, False, False, False)
            batch(B - 1, 1, B // 2 - 1, False, False, True)
            dve.wait_ge(rows_in[1], 16 * B)
            dve.wait_ge(xres_done, B)
            dve.wait_ge(y_done, 2 * B - 1)
            dve.wait_ge(y_out[1], 16 * (B - 1))
            for half, bank in enumerate((misc, O)):
                cols = slice(half * GN // 2, (half + 1) * GN // 2)
                dve.wait_ge(last_av, half + 1)
                nc.vector.tensor_tensor(by_tile(attn[:, 1, :])[:, LAST[half], :],
                                        bank[:, 0:GN // 2].rearrange("c (t n) -> c t n", t=GT // 2),
                                        inverses(1)[:, LAST[half], :], ALU.mult).then_inc(tail_step, 1)
                dve.wait_ge(tail_step, half + 1)
                nc.vector.tensor_tensor(y[:, 1, cols], attn[:, 1, cols],
                                        xres[:, 1, GN + cols.start:GN + cols.stop], ALU.add).then_inc(y_done, 1)


_INS = ['x', 'L0_conv_gn_w', 'L0_conv_gn_b', 'L0_conv_wq', 'L0_conv_bq', 'L0_conv_wk', 'L0_conv_bk',
        'L0_conv_wv', 'L0_conv_bv', 'L0_conv_wo', 'L0_conv_bo']
_OUTS = [((8, 128, 32, 32), 'float32')]


def kernel(**inputs):
    import numpy as _np
    import concourse.bacc as _bacc
    from concourse import mybir as _mybir
    from concourse.bass_utils import run_bass_kernel_spmd as _run

    nc = _bacc.Bacc("TRN2", target_bir_lowering=False, num_devices=1)
    arrays, args = {}, []
    for name in _INS:
        a = _np.ascontiguousarray(inputs[name])
        arrays[f"in_{name}_dram"] = a
        args.append(nc.dram_tensor(f"in_{name}_dram", a.shape, _mybir.dt.from_np(a.dtype), kind="ExternalInput").ap())
    for i, (shape, dtype) in enumerate(_OUTS):
        dt = _mybir.dt.from_np(_np.dtype(dtype))
        args.append(nc.dram_tensor(f"out_{i}_dram", shape, dt, kind="ExternalOutput").ap())
    groupnorm_attention_kernel(nc, *args)
    r = _run(nc, [arrays], core_ids=[0])
    return r.results[0]["out_0_dram"]
```
